# Optimizing a Trainium2 kernel written in Bass

```python
import numpy as np
import jax
import jax.numpy as jnp

def _softmax(x, axis=-1):
    return jax.nn.softmax(x, axis=axis)

def _gelu(x):
    return jax.nn.gelu(x, approximate=True)

def _silu(x):
    return jax.nn.silu(x)

def _sigmoid(x):
    return jax.nn.sigmoid(x)

def _layernorm(x, axis=-1, eps=1e-05):
    m = jnp.mean(x, axis=axis, keepdims=True)
    v = jnp.var(x, axis=axis, keepdims=True)
    return (x - m) / jnp.sqrt(v + eps)

def _scatter_add(tgt, idx, src, axis=0):
    return tgt.at[idx].add(src)

def _segment_sum(src, seg, n):
    return jax.ops.segment_sum(src, seg, n)
kernel_name = 'mk_adj_resnorm_d4_adj_r2_0d792c'

def setup_inputs(seed: int=0):
    np.random.seed(seed)
    _w = jnp.asarray

    def _rec_inputs():
        import jax
        import jax.numpy as jnp
        _gk = jax.random.key(seed)
        x = -0.000929 + 1 * jax.random.normal(jax.random.fold_in(_gk, 1), (4096, 128), jnp.float32)
        _a = jax.random.bernoulli(jax.random.fold_in(_gk, 2), 0.000976562, (4096, 4096))
        _a = jnp.logical_or(_a, jnp.swapaxes(_a, -1, -2))
        _a = jnp.logical_or(_a, jnp.eye(4096, dtype=bool))
        _af = _a.astype(jnp.float32)
        _af = _af * jax.random.uniform(jax.random.fold_in(_gk, 3), (4096, 4096), jnp.float32, 0.05, 1)
        adj = _af
        return (x, adj)
    x, adj = _rec_inputs()

    def _L0_gnn_setup():
        import jax, jax.numpy as jnp
        import numpy as np
        N = 4096
        F_IN = 128
        F_OUT = 128
        key = jax.random.key(seed)
        k1, k2, k3, k4, k5 = jax.random.split(key, 5)
        x = jax.random.normal(k1, (N, F_IN), dtype=jnp.float32)
        adj = jax.random.uniform(k2, (N, N), dtype=jnp.float32)
        kernel = jax.random.normal(k3, (F_IN, F_OUT), dtype=jnp.float32) * 0.05
        bias = jax.random.normal(k4, (F_OUT,), dtype=jnp.float32) * 0.05
        beta = jax.random.uniform(k5, (N,), dtype=jnp.float32)
        return {'x': x, 'adj': adj, 'kernel': kernel, 'bias': bias, 'beta': beta}
    _L0_gnn_all = _L0_gnn_setup()
    _L0_gnn_in = {k: v for k, v in _L0_gnn_all.items() if k in ('kernel', 'bias', 'beta')}
    del _L0_gnn_all

    def _L1_gnn_setup():
        import jax, jax.numpy as jnp
        import numpy as np
        N = 4096
        D = 128

        def _xavier(key, shape):
            fan_in, fan_out = shape
            limit = float(np.sqrt(6.0 / (fan_in + fan_out)))
            return jax.random.uniform(key, shape, jnp.float32, -limit, limit)
        key = jax.random.key(seed)
        kH, kA, k1, k2, k3, k4 = jax.random.split(key, 6)
        return {'H': jax.random.normal(kH, (N, D), jnp.float32), 'adj': jax.random.uniform(kA, (N, N), jnp.float32), 'W_l': _xavier(k1, (D, D)), 'W_r': _xavier(k2, (D, D)), 'W_h': _xavier(k3, (D, D)), 'W_g': _xavier(k4, (D, D)), 'gamma': jnp.zeros((1,), jnp.float32)}
    _L1_gnn_all = _L1_gnn_setup()
    _L1_gnn_in = {k: v for k, v in _L1_gnn_all.items() if k in ('W_l', 'W_r', 'W_h', 'W_g', 'gamma')}
    del _L1_gnn_all

    def _L2_gnn_setup():
        import jax, jax.numpy as jnp
        import numpy as np
        N = 4096
        F_IN = 128
        F_OUT = 128
        BLOCK = 64

        def _graph_pool(out, adj):
            neg = jnp.asarray(jnp.finfo(out.dtype).min, out.dtype)

            def body(_, adj_blk):
                masked = jnp.where(adj_blk[:, :, None] != 0, out[None, :, :], neg)
                return (None, jnp.max(masked, axis=1))
            _, blocks = jax.lax.scan(body, None, adj.reshape(N // BLOCK, BLOCK, N))
            return blocks.reshape(N, out.shape[-1])
        key = jax.random.key(seed)
        k_in, k_adj, k_w, k_b = jax.random.split(key, 4)
        x = jax.random.normal(k_in, (N, F_IN), dtype=jnp.float32)
        adj = (jax.random.uniform(k_adj, (N, N)) < 0.01).astype(jnp.float32)
        adj = adj.at[jnp.arange(N), jnp.arange(N)].set(1.0)
        stdv = 1.0 / np.sqrt(F_OUT)
        weight = jax.random.uniform(k_w, (F_IN, F_OUT), minval=-stdv, maxval=stdv, dtype=jnp.float32)
        bias = jax.random.uniform(k_b, (F_OUT,), minval=-stdv, maxval=stdv, dtype=jnp.float32)
        return {'input': x, 'adj': adj, 'weight': weight, 'bias': bias}
    _L2_gnn_all = _L2_gnn_setup()
    _L2_gnn_in = {k: v for k, v in _L2_gnn_all.items() if k in ('weight', 'bias')}
    del _L2_gnn_all

    def _L3_gnn_setup():
        import jax, jax.numpy as jnp
        import numpy as np
        N = 8192
        IN_DIM = 128
        OUT_DIM = 128

        def _message(X, A, W):
            deg = jnp.sum(A, axis=1, keepdims=True)
            A_norm = A / jnp.where(deg > 0, deg, 1.0)
            return A_norm @ X @ W
        key = jax.random.key(seed)
        k1, k2, k3, k4 = jax.random.split(key, 4)
        X = jax.random.normal(k1, (N, IN_DIM), dtype=jnp.float32)
        A = jax.random.uniform(k2, (N, N), dtype=jnp.float32)
        W_in = jax.random.normal(k3, (IN_DIM, OUT_DIM), dtype=jnp.float32) / np.sqrt(IN_DIM)
        W_out = jax.random.normal(k4, (IN_DIM, OUT_DIM), dtype=jnp.float32) / np.sqrt(IN_DIM)
        return {'X': X, 'A': A, 'W_in': W_in, 'W_out': W_out}
    _L3_gnn_all = _L3_gnn_setup()
    _L3_gnn_in = {k: v for k, v in _L3_gnn_all.items() if k in ('W_in', 'W_out')}
    del _L3_gnn_all
    return {'x': x, 'adj': adj, 'L0_gnn_kernel': _L0_gnn_in['kernel'], 'L0_gnn_bias': _L0_gnn_in['bias'], 'L0_gnn_beta': _L0_gnn_in['beta'], 'L1_gnn_W_l': _L1_gnn_in['W_l'], 'L1_gnn_W_r': _L1_gnn_in['W_r'], 'L1_gnn_W_h': _L1_gnn_in['W_h'], 'L1_gnn_W_g': _L1_gnn_in['W_g'], 'L1_gnn_gamma': _L1_gnn_in['gamma'], 'L2_gnn_weight': _L2_gnn_in['weight'], 'L2_gnn_bias': _L2_gnn_in['bias'], 'L3_gnn_W_in': _L3_gnn_in['W_in'], 'L3_gnn_W_out': _L3_gnn_in['W_out']}

def reference(x, adj, L0_gnn_kernel, L0_gnn_bias, L0_gnn_beta, L1_gnn_W_l, L1_gnn_W_r, L1_gnn_W_h, L1_gnn_W_g, L1_gnn_gamma, L2_gnn_weight, L2_gnn_bias, L3_gnn_W_in, L3_gnn_W_out):
    import jax
    import jax.numpy as jnp

    def _L0_gnn_ref(x, adj, kernel, bias, beta):
        import jax, jax.numpy as jnp
        import numpy as np
        N = 4096
        F_IN = 128
        F_OUT = 128
        inv_deg = 1.0 / (jnp.sum(adj, axis=1) + beta)
        agg = adj @ x + beta[:, None] * x
        out = inv_deg[:, None] * agg @ kernel + bias
        return out

    def _L1_gnn_ref(H, adj, W_l, W_r, W_h, W_g, gamma):
        import jax, jax.numpy as jnp
        import numpy as np
        N = 4096
        D = 128

        def _xavier(key, shape):
            fan_in, fan_out = shape
            limit = float(np.sqrt(6.0 / (fan_in + fan_out)))
            return jax.random.uniform(key, shape, jnp.float32, -limit, limit)
        H_l = H @ W_l
        H_r = H @ W_r
        S = H_l @ H_r.T
        beta = jax.nn.softmax(S, axis=-1)
        B = beta @ H
        O = B @ W_h @ W_g
        return adj @ H + gamma * O

    def _L2_gnn_ref(input, adj, weight, bias):
        import jax, jax.numpy as jnp
        import numpy as np
        N = 4096
        F_IN = 128
        F_OUT = 128
        BLOCK = 64

        def _graph_pool(out, adj):
            neg = jnp.asarray(jnp.finfo(out.dtype).min, out.dtype)

            def body(_, adj_blk):
                masked = jnp.where(adj_blk[:, :, None] != 0, out[None, :, :], neg)
                return (None, jnp.max(masked, axis=1))
            _, blocks = jax.lax.scan(body, None, adj.reshape(N // BLOCK, BLOCK, N))
            return blocks.reshape(N, out.shape[-1])
        h = input @ weight
        out = jnp.maximum(adj @ h + bias, 0.0)
        return _graph_pool(out, adj)

    def _L3_gnn_ref(X, A, W_in, W_out):
        import jax, jax.numpy as jnp
        import numpy as np
        N = 8192
        IN_DIM = 128
        OUT_DIM = 128

        def _message(X, A, W):
            deg = jnp.sum(A, axis=1, keepdims=True)
            A_norm = A / jnp.where(deg > 0, deg, 1.0)
            return A_norm @ X @ W
        X_in = _message(X, A, W_in)
        X_out = _message(X, A.T, W_out)
        return X_in + X_out
    x = _layernorm(x + _L0_gnn_ref(x, adj, L0_gnn_kernel, L0_gnn_bias, L0_gnn_beta), axis=-1)
    x = _layernorm(x + _L1_gnn_ref(x, adj, L1_gnn_W_l, L1_gnn_W_r, L1_gnn_W_h, L1_gnn_W_g, L1_gnn_gamma), axis=-1)
    x = _layernorm(x + _L2_gnn_ref(x, adj, L2_gnn_weight, L2_gnn_bias), axis=-1)
    x = _layernorm(x + _L3_gnn_ref(x, adj, L3_gnn_W_in, L3_gnn_W_out), axis=-1)
    return x

_drawn_inputs = setup_inputs


def setup_inputs(seed=0):
    import zlib

    import numpy as np

    out = dict(_drawn_inputs(seed))
    spreads = {}
    factors = {}
    for name, (base, spread) in spreads.items():
        noise = np.random.default_rng([zlib.crc32(name.encode()), seed]).standard_normal(out[name].shape)
        drawn = base * np.exp(spread * noise) if base else spread * noise
        out[name] = jnp.asarray(drawn.astype(out[name].dtype))
    for name, factor in factors.items():
        out[name] = (out[name] * factor).astype(out[name].dtype)
    return out
```

```python
from contextlib import ExitStack

import concourse.bass as bass
from concourse import mybir

F32 = mybir.dt.float32
BF16 = mybir.dt.bfloat16
ALU = mybir.AluOpType
ACT = mybir.ActivationFunctionType
AX = mybir.AxisListType

P = 128
BANK = 512
EPS = 1e-5
LOWEST = -3.4028234663852886e38


def bcast(ap, n):
    return ap.unsqueeze(2).broadcast_to((ap.shape[0], ap.shape[1], n))


def wait_apart(eng, sem, value, passed):
    eng.wait_ge(sem, value)
    eng.sem_inc(passed, 1)


class Count:

    def __init__(self, base=0):
        self.base, self.n = base, 0

    def up(self, k=1):
        self.n += k
        return k

    @property
    def now(self):
        return self.base + self.n


def build(nc, adj, adjT, xin, xT, K0, bias0, beta, Wl, Wr, Wh, Wg, gamma, W2, bias2, Win, Wout, out):
    N = adj.shape[0]
    T = N // P
    GW = 2 * BANK
    G = N // GW
    TG = GW // P
    Q = 4
    M = T // Q
    RING = 4

    with ExitStack() as ctx:
        def sb(name, shape, dt=F32, stack=ctx):
            return stack.enter_context(nc.sbuf_tensor(name, shape, dt))

        def sem(name):
            return ctx.enter_context(nc.semaphore(name))

        ps = ctx.enter_context(nc.psum_tensor("ps", [P, 8, BANK], F32))

        passed, passed_pe = sem("passed"), sem("passed_pe")
        xa = sb("xa", [P, T, P])
        xb = sb("xb", [P, T, P])
        res = sb("res", [P, T, P])
        ident = sb("ident", [P, P])
        ones = sb("ones", [P, P])
        k0 = sb("k0", [P, P])
        wl = sb("wl", [P, P])
        wr = sb("wr", [P, P])
        wh = sb("wh", [P, P])
        wg = sb("wg", [P, P])
        w2 = sb("w2", [P, P])
        win = sb("win", [P, P])
        wout = sb("wout", [P, P])
        bias0b = sb("bias0b", [P, P])
        bias2b = sb("bias2b", [P, P])
        gam = sb("gam", [P, 1])
        beta_sb = sb("beta_sb", [P, T])
        rowdeg = sb("rowdeg", [P, T])
        count = sb("count", [P, T])

        def prologue(b1, xt):
            loaded, made, xk_ready, v_own, xk_used = (
                sem(n) for n in ("pro_loaded", "pro_made", "pro_xk", "pro_v", "pro_xk_used"))
            loads = [(xt[:], xT), (k0[:], K0), (xa[:].rearrange("p t f -> p (t f)"), xin), (beta_sb[:], beta),
                     (bias0b[:], bias0.partition_broadcast(P)), (bias2b[:], bias2.partition_broadcast(P)),
                     (gam[:], gamma.partition_broadcast(P)),
                     (wl[:], Wl), (wr[:], Wr), (wh[:], Wh), (wg[:], Wg), (w2[:], W2), (win[:], Win), (wout[:], Wout)]
            with nc.Block(no_gpsimd_drain=True) as block:
                @block.sync
                def _(sp):
                    for dst, src in loads:
                        sp.dma_start(dst, src).then_inc(loaded, 16)
                    sp.wait_ge(loaded, 16 * len(loads))

                @block.gpsimd
                def _(pool):
                    nc.gpsimd.memset(ones[:], 1.0).then_inc(made, 1)
                    pool.wait_ge(made, 1)
                    nc.gpsimd.affine_select(out=ident[:], in_=ones[:], compare_op=ALU.is_equal, fill=0.0, base=0,
                                            pattern=[[-1, P]], channel_multiplier=1).then_inc(made, 1)
                    pool.wait_ge(made, 2)

                @block.tensor
                def _(pe):
                    pe.wait_ge(loaded, 16 * len(loads))
                    for t in range(T):
                        ins = pe.matmul(ps[:, t // 4, (t % 4) * P:(t % 4 + 1) * P], xt[:, t * P:(t + 1) * P], k0[:],
                                        start=True, stop=True)
                        if t % 4 == 3:
                            ins.then_inc(xk_ready, 1)

                @block.vector
                def _(dve):
                    dve.wait_ge(loaded, 16 * len(loads))
                    for b in range(T // 4):
                        s = slice(4 * b, 4 * b + 4)
                        nc.vector.tensor_tensor(res[:, s, :], xa[:, s, :],
                                                bias0b[:].unsqueeze(1).broadcast_to((P, 4, P)), ALU.add)
                        dve.wait_ge(xk_ready, b + 1)
                        nc.vector.tensor_tensor(b1[:, s, :], ps[:, b, :].rearrange("p (t f) -> p t f", f=P),
                                                bcast(beta_sb[:, s], P), ALU.mult)

        def aggregate(name, stream, x, right, finish, steps, degree=None, store=None, norm=True):
            view = stream.rearrange("(m q p) (g w) -> m g p q w", q=Q, p=P, w=GW)
            loaded = [sem(f"{name}_loaded{s}") for s in range(RING)]
            slot_used, agg_copied, y_ready, y_used, summed, deg_acc, deg_ready, v_own, done, stored, var_ready, std_ready = (
                sem(f"{name}_{n}") for n in ("slot_used", "agg_copied", "y_ready", "y_used", "summed",
                                             "deg_acc", "deg_ready", "v_own", "done", "stored",
                                             "var_ready", "std_ready"))
            with ExitStack() as own:
                ring = sb(f"{name}_ring", [P, RING, Q, GW], F32, own)
                aggT = sb(f"{name}_aggT", [P, 2, GW], F32, own)
                if degree is not None:
                    pair = sb(f"{name}_pair", [P, 2, GW], F32, own)
                    acc = sb(f"{name}_acc", [P, GW], F32, own)
                y = ps[:, 4:6, :].rearrange("p b (t f) -> p (b t) f", f=P)
                work = sb(f"{name}_work", [P, 2, TG, P], F32, own)
                stats = sb(f"{name}_stats", [P, TG, 6], F32, own)
                mv = sb(f"{name}_mv", [P, TG, 2], F32, own)
                rstd = sb(f"{name}_rstd", [P, TG], F32, own)
                block = own.enter_context(nc.Block(no_gpsimd_drain=True))

                @block.sync
                def _(sp):
                    with sp.Fori(0, G // 2) as it:
                        for h in range(2):
                            for m in range(M):
                                sp.wait_ge(slot_used, (it * 2 + h) * M + m + 1)
                                if degree is not None:
                                    sp.wait_ge(summed, (it * 2 + h) * M + m + 1)
                                sp.dma_start(ring[:, m % RING], view[m, it * 2 + h]).then_inc(loaded[m % RING], 16)

                @block.tensor
                def _(pe):
                    pe.sem_inc(slot_used, RING)
                    with pe.Fori(0, G // 2) as it:
                        for h in range(2):
                            g = it * 2 + h
                            for m in range(M):
                                pe.wait_ge(loaded[m % RING], (g * (M // RING) + m // RING + 1) * 16)
                                if m == 0:
                                    pe.wait_ge(agg_copied, g + 1)
                                for q in range(Q):
                                    c = m * Q + q
                                    for b in range(2):
                                        ins = pe.matmul(ps[:, 2 * h + b, :], x[:, c, :],
                                                        ring[:, m % RING, q, b * BANK:(b + 1) * BANK],
                                                        start=c == 0, stop=c == T - 1)
                                ins.then_inc(slot_used, 1)
                            if degree is not None:
                                pe.wait_ge(deg_acc, g + 1)
                                for k in range(TG):
                                    ins = pe.matmul(ps[:, 6, k:k + 1], acc[:, k * P:(k + 1) * P], ones[:, 0:1],
                                                    start=True, stop=True)
                                ins.then_inc(deg_ready, 1)
                            pe.wait_ge(agg_copied, g + 3)
                            pe.wait_ge(y_used, g + 1)
                            for k in range(TG):
                                ins = pe.matmul(y[:, k, :], aggT[:, h, k * P:(k + 1) * P], right[:],
                                                start=True, stop=True)
                            ins.then_inc(y_ready, 1)

                @block.scalar
                def _(act):
                    act.sem_inc(agg_copied, 2)
                    with act.Fori(0, G // 2) as it:
                        for h in range(2):
                            act.wait_ge(slot_used, (it * 2 + h) * M + M + RING)
                            nc.scalar.copy(aggT[:, h, :], ps[:, 2 * h:2 * h + 2, :].rearrange("p b w -> p (b w)")
                                           ).then_inc(agg_copied, 1)
                            if norm:
                                act.wait_ge(var_ready, it * 2 + h + 1)
                                nc.scalar.activation(rstd[:], rstd[:], ACT.Sqrt).then_inc(std_ready, 1)

                @block.vector
                def _(dve):
                    dve.sem_inc(y_used, 1)
                    summing = 3 * M - 2 + 1 if degree is not None else 0
                    if degree is not None:
                        dve.sem_inc(summed, RING)
                    with dve.Fori(0, G // 2) as it:
                        for h in range(2):
                            g = it * 2 + h
                            own_n = Count(g * (summing + steps))
                            if degree is not None:
                                for m in range(M):
                                    dve.wait_ge(loaded[m % RING], (g * (M // RING) + m // RING + 1) * 16)
                                    r = ring[:, m % RING]
                                    nc.vector.tensor_tensor(pair[:, 0, :], r[:, 0, :], r[:, 1, :], ALU.add
                                                            ).then_inc(v_own, own_n.up())
                                    nc.vector.tensor_tensor(pair[:, 1, :], r[:, 2, :], r[:, 3, :], ALU.add
                                                            ).then_inc(summed, 1)
                                    dve.wait_ge(summed, g * M + m + 1 + RING)
                                    dve.wait_ge(v_own, own_n.now)
                                    if m == 0:
                                        nc.vector.tensor_tensor(acc[:], pair[:, 0, :], pair[:, 1, :], ALU.add
                                                                ).then_inc(v_own, own_n.up())
                                        dve.wait_ge(v_own, own_n.now)
                                        continue
                                    nc.vector.tensor_tensor(pair[:, 0, :], pair[:, 0, :], pair[:, 1, :], ALU.add
                                                            ).then_inc(v_own, own_n.up())
                                    dve.wait_ge(v_own, own_n.now)
                                    last = nc.vector.tensor_tensor(acc[:], acc[:], pair[:, 0, :], ALU.add)
                                    if m < M - 1:
                                        last.then_inc(v_own, own_n.up())
                                        dve.wait_ge(v_own, own_n.now)
                                    else:
                                        last.then_inc(deg_acc, 1)
                                dve.wait_ge(deg_ready, g + 1)
                                nc.vector.tensor_copy(degree[:, bass.ds(g * TG, TG)], ps[:, 6, 0:TG]
                                                      ).then_inc(v_own, own_n.up())
                                dve.wait_ge(v_own, own_n.now)
                                assert own_n.n == summing, (own_n.n, summing)
                            dve.wait_ge(y_ready, g + 1)
                            if store is not None:
                                dve.wait_ge(stored, g * 16)
                            finish(dve, g, y, y_used, v_own, own_n, work, stats, mv, rstd,
                                   (var_ready, std_ready, g + 1), done)
                            assert own_n.n == summing + steps, (own_n.n, summing, steps)

                if store is not None:
                    rows = store.rearrange("(g t p) f -> g p t f", t=TG, p=P)

                    @block.gpsimd
                    def _(pool):
                        with pool.Fori(0, G) as g:
                            pool.wait_ge(done, g + 1)
                            pool.dma_start(rows[g], work[:, 1]).then_inc(stored, 16)
                        pool.wait_ge(stored, 16 * G)

        NORM_STEPS = 2 * TG + 3

        def normalize(dve, v_own, own_n, work, stats, mv, rstd, root, to, done=None):
            for k in range(TG):
                nc.vector.bn_stats(stats[:, k, :], work[:, 0, k, :]).then_inc(v_own, own_n.up())
            wait_apart(dve, v_own, own_n.now, passed)
            for k in range(TG):
                nc.vector.bn_aggr(mv[:, k, :], stats[:, k, :]).then_inc(v_own, own_n.up())
            dve.wait_ge(v_own, own_n.now)
            var_ready, std_ready, turn_no = root
            nc.vector.tensor_scalar(rstd[:], mv[:, :, 1], EPS, None, ALU.add).then_inc(var_ready, 1)
            nc.vector.tensor_tensor(work[:, 0], work[:, 0], bcast(mv[:, :, 0], P), ALU.subtract
                                    ).then_inc(v_own, own_n.up())
            dve.wait_ge(std_ready, turn_no)
            nc.vector.reciprocal(rstd[:], rstd[:]).then_inc(v_own, own_n.up())
            dve.wait_ge(v_own, own_n.now)
            last = nc.vector.tensor_tensor(to, work[:, 0], bcast(rstd[:], P), ALU.mult)
            if done is not None:
                last.then_inc(done[0], 1)
                dve.wait_ge(done[0], done[1])
            else:
                last.then_inc(v_own, own_n.up())
                dve.wait_ge(v_own, own_n.now)

        with ExitStack() as own:
            b1 = sb("b1", [P, T, P], F32, own)
            with ExitStack() as inner:
                xt = sb("xt", [P, N], F32, inner)
                prologue(b1, xt)

            inv = sb("inv", [P, TG], F32, own)

            def finish0(dve, g, y, y_used, v_own, n, work, stats, mv, rstd, root, done):
                tiles = bass.ds(g * TG, TG)
                w = work[:, 0]
                nc.vector.tensor_tensor(inv[:], rowdeg[:, tiles], beta_sb[:, tiles], ALU.add).then_inc(v_own, n.up())
                dve.wait_ge(v_own, n.now)
                nc.vector.reciprocal(inv[:], inv[:]).then_inc(v_own, n.up())
                nc.vector.tensor_tensor(w, y, b1[:, tiles, :], ALU.add).then_inc(y_used, 1)
                dve.wait_ge(y_used, g + 2)
                dve.wait_ge(v_own, n.now)
                nc.vector.tensor_tensor(w, w, bcast(inv[:], P), ALU.mult).then_inc(v_own, n.up())
                dve.wait_ge(v_own, n.now)
                nc.vector.tensor_tensor(w, w, res[:, tiles, :], ALU.add).then_inc(v_own, n.up())
                dve.wait_ge(v_own, n.now)
                normalize(dve, v_own, n, work, stats, mv, rstd, root, xb[:, tiles, :])

            aggregate("l0", adjT, xa, k0, finish0, 4 + NORM_STEPS, degree=rowdeg)

        def project(x, HT, HlT, HrT):
            turned, ht_ready, l_ready, l_copied, r_ready, r_copied = (
                sem(f"proj_{n}") for n in ("turned", "ht_ready", "l_ready", "l_copied", "r_ready", "r_copied"))
            with nc.Block(no_gpsimd_drain=True) as block:
                @block.tensor
                def _(pe):
                    for b in range(8):
                        for k in range(4):
                            ins = pe.matmul(ps[:, b, k * P:(k + 1) * P], x[:, 4 * b + k, :], ident[:],
                                            start=True, stop=True)
                        ins.then_inc(turned, 1)
                    for b in range(8):
                        pe.wait_ge(ht_ready, b + 1)
                        pe.matmul(ps[:, b, :], wl[:], HT[:, b * BANK:(b + 1) * BANK], start=True, stop=True
                                  ).then_inc(l_ready, 1)
                    for b in range(8):
                        pe.wait_ge(l_copied, b + 1)
                        pe.matmul(ps[:, b, :], wr[:], HT[:, b * BANK:(b + 1) * BANK], start=True, stop=True
                                  ).then_inc(r_ready, 1)

                @block.scalar
                def _(act):
                    for b in range(8):
                        act.wait_ge(turned, b + 1)
                        nc.scalar.copy(HT[:, b * BANK:(b + 1) * BANK], ps[:, b, :]).then_inc(ht_ready, 1)
                    for b in range(8):
                        act.wait_ge(r_ready, b + 1)
                        nc.scalar.copy(HrT[:, b * BANK:(b + 1) * BANK], ps[:, b, :]).then_inc(r_copied, 1)

                @block.vector
                def _(dve):
                    for b in range(8):
                        dve.wait_ge(l_ready, b + 1)
                        nc.vector.tensor_copy(HlT[:, b * BANK:(b + 1) * BANK], ps[:, b, :]).then_inc(l_copied, 1)

        def row_maxima(HlT, HrT, rowmax):
            lt_ready, own_v = sem("rm_lt_ready"), sem("rm_own")
            scored = [sem("rm_scored0"), sem("rm_scored1")]
            taken = [sem("rm_taken0"), sem("rm_taken1")]
            with ExitStack() as own:
                lt = sb("lt", [P, 2, P], F32, own)
                mx = sb("mx", [P, 2, 2], F32, own)
                block = own.enter_context(nc.Block(no_gpsimd_drain=True))

                @block.scalar
                def _(act):
                    with act.Fori(0, T // 2) as it:
                        for h in range(2):
                            act.wait_ge(scored[1], it * 2 + h + 1)
                            nc.scalar.copy(lt[:, h, :], HlT[:, bass.ds((it * 2 + h) * P, P)]).then_inc(lt_ready, 1)

                @block.tensor
                def _(pe):
                    pe.sem_inc(scored[1], 2)
                    with pe.Fori(0, T // 2) as it:
                        for h in range(2):
                            t = it * 2 + h
                            pe.wait_ge(lt_ready, t + 1)
                            for u in range(2):
                                pe.wait_ge(taken[u], t + 1)
                                for b in range(4 * u, 4 * u + 4):
                                    ins = pe.matmul(ps[:, b, :], lt[:, h, :], HrT[:, b * BANK:(b + 1) * BANK],
                                                    start=True, stop=True)
                                ins.then_inc(scored[u], 1)

                @block.vector
                def _(dve):
                    dve.sem_inc(taken[0], 1)
                    dve.sem_inc(taken[1], 1)
                    with dve.Fori(0, T // 2) as it:
                        for h in range(2):
                            t = it * 2 + h
                            for u in range(2):
                                dve.wait_ge(scored[u], t + 1 + 2 * u)
                                nc.vector.tensor_reduce(mx[:, h, u:u + 1],
                                                        ps[:, 4 * u:4 * u + 4, :].rearrange("p b w -> p (b w)"),
                                                        AX.X, ALU.max).then_inc(taken[u], 1)
                            for u in range(2):
                                dve.wait_ge(taken[u], t + 2)
                            nc.vector.tensor_tensor(rowmax[:, bass.ds(t, 1)], mx[:, h, 0:1], mx[:, h, 1:2], ALU.max
                                                    ).then_inc(own_v, 1)
                            dve.wait_ge(own_v, t + 1)

        def spread_maxima(rowmax, mb):
            spread, made, copied = sem("sp_spread"), sem("sp_made"), sem("sp_copied")
            with ExitStack() as own:
                diag = sb("diag", [P, 2, 4, P], F32, own)
                block = own.enter_context(nc.Block(no_gpsimd_drain=True))

                @block.vector
                def _(dve):
                    for b in range(8):
                        if b >= 2:
                            dve.wait_ge(spread, b - 1)
                        nc.vector.tensor_tensor(diag[:, b % 2], ident[:].unsqueeze(1).broadcast_to((P, 4, P)),
                                                bcast(rowmax[:, 4 * b:4 * b + 4], P), ALU.mult).then_inc(made, 1)

                @block.tensor
                def _(pe):
                    for b in range(8):
                        pe.wait_ge(made, b + 1)
                        pe.matmul(ps[:, b, :], ones[:], diag[:, b % 2].rearrange("p t f -> p (t f)"),
                                  start=True, stop=True).then_inc(spread, 1)

                @block.scalar
                def _(act):
                    for b in range(8):
                        act.wait_ge(spread, b + 1)
                        nc.scalar.copy(mb[:, b * BANK:(b + 1) * BANK], ps[:, b, :]).then_inc(copied, 1)

        def attend(x, HlT, HrT, mb):
            R = 4
            LAG = 2
            st_ready, pt_ready, sum_done, pv_done, s_ready, bt_copied, z_ready, z_copied, o_ready, o_used, own_v = (
                sem(f"at_{n}") for n in ("st_ready", "pt_ready", "sum_done", "pv_done", "s_ready", "bt_copied",
                                         "z_ready", "z_copied", "o_ready", "o_used", "own"))
            with ExitStack() as own:
                st = sb("st", [P, R, BANK], F32, own)
                pt = sb("pt", [P, R, BANK], F32, own)
                sumP = sb("sumP", [P, BANK], F32, own)
                btS = sb("btS", [P, BANK], F32, own)
                zS = sb("zS", [P, BANK], F32, own)
                rl = sb("rl", [P, 4], F32, own)
                w4 = sb("w4", [P, 4, P], F32, own)
                block = own.enter_context(nc.Block(no_gpsimd_drain=True))

                @block.tensor
                def _(pe):
                    pe.sem_inc(pv_done, R)
                    with pe.Fori(0, N // BANK) as ig:
                        for s in range(T + LAG):
                            if s < T:
                                pe.wait_ge(st_ready, ig * T + s + 1)
                                pe.matmul(ps[:, s % R, :], HrT[:, s * P:(s + 1) * P], HlT[:, bass.ds(ig * BANK, BANK)],
                                          start=True, stop=True).then_inc(s_ready, 1)
                            if s >= LAG:
                                j = s - LAG
                                pe.wait_ge(pt_ready, ig * T + j + 1 + R)
                                if j == 0:
                                    pe.wait_ge(bt_copied, ig + 1)
                                pe.matmul(ps[:, 4, :], x[:, j, :], pt[:, j % R, :], start=j == 0, stop=j == T - 1
                                          ).then_inc(pv_done, 1)
                        pe.wait_ge(bt_copied, ig + 2)
                        pe.matmul(ps[:, 5, :], wh[:], btS[:], start=True, stop=True).then_inc(z_ready, 1)
                        pe.wait_ge(o_used, ig + 1)
                        pe.wait_ge(sum_done, ig * T + T + R)
                        for k in range(4):
                            pe.matmul(ps[:, 7, k:k + 1], sumP[:, k * P:(k + 1) * P], ones[:, 0:1],
                                      start=True, stop=True)
                        pe.wait_ge(z_copied, ig + 1)
                        for k in range(4):
                            ins = pe.matmul(ps[:, 6, k * P:(k + 1) * P], zS[:, k * P:(k + 1) * P], wg[:],
                                            start=True, stop=True)
                        ins.then_inc(o_ready, 1)

                @block.scalar
                def _(act):
                    act.sem_inc(pt_ready, R)
                    act.sem_inc(bt_copied, 1)
                    with act.Fori(0, N // BANK) as ig:
                        for s in range(T):
                            act.wait_ge(st_ready, ig * T + s + 1 + R)
                            act.wait_ge(pv_done, ig * T + s + 1)
                            act.wait_ge(sum_done, ig * T + s + 1)
                            nc.scalar.activation(pt[:, s % R, :], st[:, s % R, :], ACT.Exp).then_inc(pt_ready, 1)
                        act.wait_ge(pv_done, ig * T + T + R)
                        nc.scalar.copy(btS[:], ps[:, 4, :]).then_inc(bt_copied, 1)
                        act.wait_ge(z_ready, ig + 1)
                        nc.scalar.copy(zS[:], ps[:, 5, :]).then_inc(z_copied, 1)

                @block.vector
                def _(dve):
                    dve.sem_inc(st_ready, R)
                    dve.sem_inc(sum_done, R)
                    dve.sem_inc(o_used, 1)
                    with dve.Fori(0, N // BANK) as ig:
                        for s in range(T + LAG):
                            if s < T:
                                dve.wait_ge(s_ready, ig * T + s + 1)
                                dve.wait_ge(pt_ready, ig * T + s + 1)
                                nc.vector.tensor_tensor(st[:, s % R, :], ps[:, s % R, :],
                                                        mb[:, bass.ds(ig * BANK, BANK)], ALU.subtract
                                                        ).then_inc(st_ready, 1)
                            if s >= LAG:
                                j = s - LAG
                                dve.wait_ge(pt_ready, ig * T + j + 1 + R)
                                if j == 0:
                                    nc.vector.tensor_copy(sumP[:], pt[:, 0, :]).then_inc(sum_done, 1)
                                else:
                                    dve.wait_ge(sum_done, ig * T + j + R)
                                    nc.vector.tensor_tensor(sumP[:], sumP[:], pt[:, j % R, :], ALU.add
                                                            ).then_inc(sum_done, 1)
                        tiles = bass.ds(ig * 4, 4)
                        dve.wait_ge(o_ready, ig + 1)
                        nc.vector.reciprocal(rl[:], ps[:, 7, 0:4]).then_inc(own_v, 1)
                        dve.wait_ge(own_v, ig * 3 + 1)
                        nc.vector.tensor_scalar(rl[:], rl[:], gam[:, 0:1], None, ALU.mult).then_inc(own_v, 1)
                        dve.wait_ge(own_v, ig * 3 + 2)
                        nc.vector.tensor_tensor(w4[:], ps[:, 6, :].rearrange("p (t f) -> p t f", f=P),
                                                bcast(rl[:], P), ALU.mult).then_inc(o_used, 1)
                        dve.wait_ge(o_used, ig + 2)
                        nc.vector.tensor_tensor(res[:, tiles, :], w4[:], x[:, tiles, :], ALU.add).then_inc(own_v, 1)
                        dve.wait_ge(own_v, ig * 3 + 3)

        with ExitStack() as own:
            HlT = sb("HlT", [P, N], F32, own)
            HrT = sb("HrT", [P, N], F32, own)
            with ExitStack() as inner:
                HT = sb("HT", [P, N], F32, inner)
                project(xb, HT, HlT, HrT)
            mb = sb("mb", [P, N], F32, own)
            rowmax = sb("rowmax", [P, T], F32, own)
            row_maxima(HlT, HrT, rowmax)
            spread_maxima(rowmax, mb)
            attend(xb, HlT, HrT, mb)

        def finish1(dve, g, y, y_used, v_own, n, work, stats, mv, rstd, root, done):
            tiles = bass.ds(g * TG, TG)
            nc.vector.tensor_tensor(work[:, 0], y, res[:, tiles, :], ALU.add).then_inc(y_used, 1)
            dve.wait_ge(y_used, g + 2)
            normalize(dve, v_own, n, work, stats, mv, rstd, root, xa[:, tiles, :])

        aggregate("l1", adjT, xb, ident, finish1, NORM_STEPS)

        def finish2(dve, g, y, y_used, v_own, n, work, stats, mv, rstd, root, done):
            tiles = bass.ds(g * TG, TG)
            nc.vector.tensor_tensor(work[:, 0], y, bias2b[:].unsqueeze(1).broadcast_to((P, TG, P)), ALU.add
                                    ).then_inc(y_used, 1)
            dve.wait_ge(y_used, g + 2)
            nc.vector.tensor_scalar(res[:, tiles, :], work[:, 0], 0.0, None, ALU.max).then_inc(v_own, n.up())
            dve.wait_ge(v_own, n.now)

        aggregate("l2", adjT, xa, w2, finish2, 1, norm=False)

        def turn(x, xT_sb, name):
            turned, copied = sem(f"{name}_turned"), sem(f"{name}_copied")
            with nc.Block(no_gpsimd_drain=True) as block:
                @block.tensor
                def _(pe):
                    for b in range(8):
                        for k in range(4):
                            ins = pe.matmul(ps[:, b, k * P:(k + 1) * P], x[:, 4 * b + k, :], ident[:],
                                            start=True, stop=True)
                        ins.then_inc(turned, 1)

                @block.scalar
                def _(act):
                    for b in range(8):
                        act.wait_ge(turned, b + 1)
                        nc.scalar.copy(xT_sb[:, b * BANK:(b + 1) * BANK], ps[:, b, :]).then_inc(copied, 1)

        def pool_dense(hT, RT):
            rows = adj.rearrange("(t p) j -> t p j", p=P)
            made, own_v = sem("pl_made"), sem("pl_own")
            loaded = [sem("pl_loaded0"), sem("pl_loaded1")]
            spread = [sem("pl_spread0"), sem("pl_spread1")]
            taken = [sem("pl_taken0"), sem("pl_taken1")]
            with ExitStack() as own:
                a = sb("pool_a", [P, 2, N], F32, own)
                mask = sb("pool_mask", [P, 2, N], BF16, own)
                identb = sb("identb", [P, P], BF16, own)
                junk = sb("pool_junk", [P, 2, N // 2], BF16, own)
                pm = sb("pool_pm", [P, 2], F32, own)
                block = own.enter_context(nc.Block(no_gpsimd_drain=True))

                @block.sync
                def _(sp):
                    with sp.Fori(0, T // 2) as it:
                        for h in range(2):
                            sp.wait_ge(made, it * 4 + 2 * h + 1)
                            sp.dma_start(a[:, h, :], rows[it * 2 + h]).then_inc(loaded[h], 16)

                @block.tensor
                def _(pe):
                    with pe.Fori(0, T // 2) as it:
                        for h in range(2):
                            wait_apart(pe, made, it * 4 + 2 * h + 6, passed)
                            with pe.Fori(0, P) as i:
                                n = (it * 2 + h) * P + i
                                for u in range(2):
                                    pe.wait_ge(taken[u], n + 1)
                                    for b in range(4 * u, 4 * u + 4):
                                        ins = pe.matmul(ps[:, b, :], identb[:, bass.ds(i, 1)].broadcast_to((P, P)),
                                                        mask[:, h, b * BANK:(b + 1) * BANK], start=True, stop=True)
                                    ins.then_inc(spread[u], 1)

                @block.vector
                def _(dve):
                    nc.vector.tensor_copy(identb[:], ident[:]).then_inc(made, 1)
                    dve.wait_ge(made, 1)
                    dve.sem_inc(made, 3)
                    dve.sem_inc(taken[0], 1)
                    dve.sem_inc(taken[1], 1)
                    with dve.Fori(0, T // 2) as it:
                        for h in range(2):
                            t = it * 2 + h
                            dve.wait_ge(loaded[h], (it + 1) * 16)
                            nc.vector.tensor_scalar(mask[:, h, :], a[:, h, :], 0.0, None, ALU.not_equal
                                                    ).then_inc(made, 1)
                            dve.wait_ge(made, it * 4 + 2 * h + 5)
                            nc.vector.tensor_reduce(count[:, bass.ds(t, 1)], mask[:, h, :], AX.X, ALU.add
                                                    ).then_inc(made, 1)
                            wait_apart(dve, made, it * 4 + 2 * h + 6, passed)
                            with dve.Fori(0, P) as i:
                                n = t * P + i
                                for u in range(2):
                                    wait_apart(dve, spread[u], n + 1, passed)
                                    nc.vector.tensor_tensor_reduce(
                                        out=junk[:, u, :], in0=hT[:, u * (N // 2):(u + 1) * (N // 2)],
                                        in1=ps[:, 4 * u:4 * u + 4, :].rearrange("p b w -> p (b w)"),
                                        scale=1.0, scalar=0.0, op0=ALU.mult, op1=ALU.max,
                                        accum_out=pm[:, u:u + 1]).then_inc(taken[u], 1)
                                dve.wait_ge(taken[0], n + 2)
                                dve.wait_ge(taken[1], n + 2)
                                nc.vector.tensor_tensor(RT[:, bass.ds(n, 1)], pm[:, 0:1], pm[:, 1:2], ALU.max
                                                        ).then_inc(own_v, 1)
                                dve.wait_ge(own_v, n + 1)

        def finish_pool(RT):
            turned, own_v, var_ready, std_ready = (sem(f"fp_{n}") for n in ("turned", "own", "var_ready", "std_ready"))
            with ExitStack() as own:
                work = sb("fp_work", [P, 2, TG, P], F32, own)
                stats = sb("fp_stats", [P, TG, 6], F32, own)
                mv = sb("fp_mv", [P, TG, 2], F32, own)
                rstd = sb("fp_rstd", [P, TG], F32, own)
                low = sb("fp_low", [P, T], F32, own)
                block = own.enter_context(nc.Block(no_gpsimd_drain=True))

                @block.tensor
                def _(pe):
                    for b in range(8):
                        for k in range(4):
                            t = 4 * b + k
                            ins = pe.matmul(ps[:, b, k * P:(k + 1) * P], RT[:, t * P:(t + 1) * P], ident[:],
                                            start=True, stop=True)
                        ins.then_inc(turned, 1)

                @block.vector
                def _(dve):
                    n = Count()
                    nc.vector.tensor_scalar(low[:], count[:], 0.0, LOWEST, ALU.is_equal, ALU.mult
                                            ).then_inc(own_v, n.up())
                    dve.wait_ge(own_v, n.now)
                    for g in range(G):
                        tiles = slice(g * TG, (g + 1) * TG)
                        dve.wait_ge(turned, 2 * g + 2)
                        nc.vector.tensor_tensor(work[:, 0],
                                                ps[:, 2 * g:2 * g + 2, :].rearrange("p b (t f) -> p (b t) f", f=P),
                                                bcast(low[:, tiles], P), ALU.add).then_inc(own_v, n.up())
                        dve.wait_ge(own_v, n.now)
                        nc.vector.tensor_tensor(work[:, 0], work[:, 0], xa[:, tiles, :], ALU.add
                                                ).then_inc(own_v, n.up())
                        dve.wait_ge(own_v, n.now)
                        normalize(dve, own_v, n, work, stats, mv, rstd, (var_ready, std_ready, g + 1), xb[:, tiles, :])

                @block.scalar
                def _(act):
                    for g in range(G):
                        act.wait_ge(var_ready, g + 1)
                        nc.scalar.activation(rstd[:], rstd[:], ACT.Sqrt).then_inc(std_ready, 1)

        with ExitStack() as own:
            hT = sb("hT", [P, N], F32, own)
            RT = sb("RT", [P, N], F32, own)
            turn(res, hT, "h")
            pool_dense(hT, RT)
            finish_pool(RT)

        SAFE_STEPS = 5

        def inverse_of(dve, deg, inv, spare, v_own, n):
            nc.vector.tensor_scalar(spare[:], deg, 0.0, None, ALU.is_gt).then_inc(v_own, n.up())
            dve.wait_ge(v_own, n.now)
            nc.vector.tensor_tensor(inv[:], deg, spare[:], ALU.mult).then_inc(v_own, n.up())
            nc.vector.tensor_scalar(spare[:], spare[:], -1.0, 1.0, ALU.mult, ALU.add).then_inc(v_own, n.up())
            dve.wait_ge(v_own, n.now)
            nc.vector.tensor_tensor(inv[:], inv[:], spare[:], ALU.add).then_inc(v_own, n.up())
            dve.wait_ge(v_own, n.now)
            nc.vector.reciprocal(inv[:], inv[:]).then_inc(v_own, n.up())
            dve.wait_ge(v_own, n.now)

        with ExitStack() as own:
            inv3 = sb("inv3", [P, TG], F32, own)
            spare = sb("spare3", [P, TG], F32, own)
            coldeg = sb("coldeg", [P, T], F32, own)

            def finish3(dve, g, y, y_used, v_own, n, work, stats, mv, rstd, root, done):
                tiles = bass.ds(g * TG, TG)
                inverse_of(dve, rowdeg[:, tiles], inv3, spare, v_own, n)
                nc.vector.tensor_tensor(work[:, 0], y, bcast(inv3[:], P), ALU.mult).then_inc(y_used, 1)
                dve.wait_ge(y_used, g + 2)
                nc.vector.tensor_tensor(res[:, tiles, :], work[:, 0], xb[:, tiles, :], ALU.add
                                        ).then_inc(v_own, n.up())
                dve.wait_ge(v_own, n.now)

            aggregate("l3in", adjT, xb, win, finish3, SAFE_STEPS + 1, norm=False)

            def finish4(dve, g, y, y_used, v_own, n, work, stats, mv, rstd, root, done):
                tiles = bass.ds(g * TG, TG)
                inverse_of(dve, coldeg[:, tiles], inv3, spare, v_own, n)
                nc.vector.tensor_tensor(work[:, 0], y, bcast(inv3[:], P), ALU.mult).then_inc(y_used, 1)
                dve.wait_ge(y_used, g + 2)
                nc.vector.tensor_tensor(work[:, 0], work[:, 0], res[:, tiles, :], ALU.add
                                        ).then_inc(v_own, n.up())
                dve.wait_ge(v_own, n.now)
                normalize(dve, v_own, n, work, stats, mv, rstd, root, work[:, 1], (done, g + 1))

            aggregate("l3out", adj, xb, wout, finish4, SAFE_STEPS + NORM_STEPS, degree=coldeg, store=out)


def kernel(x, adj, L0_gnn_kernel, L0_gnn_bias, L0_gnn_beta, L1_gnn_W_l, L1_gnn_W_r, L1_gnn_W_h, L1_gnn_W_g,
           L1_gnn_gamma, L2_gnn_weight, L2_gnn_bias, L3_gnn_W_in, L3_gnn_W_out):
    import numpy as np
    import concourse.bacc as bacc
    from concourse.bass_utils import run_bass_kernel_spmd

    x, adj = np.asarray(x), np.asarray(adj)
    N, D = x.shape
    tiled = x.reshape(N // P, P, D).transpose(1, 0, 2).reshape(P, -1)
    ins = {
        "adj": adj, "adjT": adj.T, "xin": tiled, "xT": x.T, "K0": L0_gnn_kernel,
        "bias0": np.asarray(L0_gnn_bias), "beta": np.asarray(L0_gnn_beta).reshape(N // P, P).T,
        "Wl": L1_gnn_W_l, "Wr": L1_gnn_W_r, "Wh": L1_gnn_W_h, "Wg": L1_gnn_W_g, "gamma": L1_gnn_gamma,
        "W2": L2_gnn_weight, "bias2": L2_gnn_bias, "Win": L3_gnn_W_in, "Wout": L3_gnn_W_out,
    }
    nc = bacc.Bacc("TRN2", target_bir_lowering=False, num_devices=1)
    arrays, args = {}, {}
    for name, a in ins.items():
        a = np.ascontiguousarray(a)
        arrays[f"in_{name}"] = a
        args[name] = nc.dram_tensor(f"in_{name}", a.shape, mybir.dt.from_np(a.dtype), kind="ExternalInput").ap()
    out = nc.dram_tensor("out_x", (N, D), F32, kind="ExternalOutput").ap()
    build(nc, out=out, **args)
    r = run_bass_kernel_spmd(nc, [arrays], core_ids=[0])
    return r.results[0]["out_x"]
```

```python
from contextlib import ExitStack

import concourse.bass as bass
from concourse import mybir

F32 = mybir.dt.float32
BF16 = mybir.dt.bfloat16
U32 = mybir.dt.uint32
ALU = mybir.AluOpType
ACT = mybir.ActivationFunctionType
AX = mybir.AxisListType

P = 128
BANK = 512
EPS = 1e-5
LOWEST = -3.4028234663852886e38


def bcast(ap, n):
    return ap.unsqueeze(2).broadcast_to((ap.shape[0], ap.shape[1], n))


def wait_apart(eng, sem, value, passed):
    eng.wait_ge(sem, value)
    eng.sem_inc(passed, 1)


class Count:

    def __init__(self, base=0):
        self.base, self.n = base, 0

    def up(self, k=1):
        self.n += k
        return k

    @property
    def now(self):
        return self.base + self.n


def build(nc, adj, adjT, xin, xT, K0, bias0, beta, Wl, Wr, Wh, Wg, gamma, W2, bias2, Win, Wout, diag, out):
    N = adj.shape[0]
    T = N // P
    GW = 2 * BANK
    G = N // GW
    TG = GW // P
    Q = 4
    M = T // Q
    RING = 4
    SEG = 8
    S = 24
    K = 12
    E = 8

    with ExitStack() as ctx:
        def sb(name, shape, dt=F32, stack=ctx):
            return stack.enter_context(nc.sbuf_tensor(name, shape, dt))

        def sem(name):
            return ctx.enter_context(nc.semaphore(name))

        ps = ctx.enter_context(nc.psum_tensor("ps", [P, 8, BANK], F32))

        passed, passed_pool, passed_pe = sem("passed"), sem("passed_pool"), sem("passed_pe")
        adj_rows = adj.rearrange("(t p) j -> t p j", p=P)
        xa = sb("xa", [P, T, P])
        xb = sb("xb", [P, T, P])
        res = sb("res", [P, T, P])
        ident = sb("ident", [P, P])
        ones = sb("ones", [P, P])
        off_diag = sb("off_diag", [P, P])
        k0 = sb("k0", [P, P])
        wl = sb("wl", [P, P])
        wr = sb("wr", [P, P])
        wh = sb("wh", [P, P])
        wg = sb("wg", [P, P])
        w2 = sb("w2", [P, P])
        win = sb("win", [P, P])
        wout = sb("wout", [P, P])
        bias0b = sb("bias0b", [P, P])
        bias2b = sb("bias2b", [P, P])
        gam = sb("gam", [P, 1])
        beta_sb = sb("beta_sb", [P, T])
        rowdeg = sb("rowdeg", [P, T])
        count = sb("count", [P, T])
        diag_sb = sb("diag_sb", [P, T])
        keys = sb("keys", [P, T, S])
        keysum = sb("keysum", [P, T])
        esel = sb("esel", [P, E])
        main_idx = sb("main_idx", [P, T + 2, K], U32)
        extra_idx = sb("extra_idx", [P, E, S - K], U32)
        emask = sb("emask", [P, E, T])
        ok = sb("ok", [P, 1], mybir.dt.int32)
        h_rows = nc.dram_tensor("h_rows", [N + 1, P], F32, kind="Internal").ap()

        zero_row = sb("zero_row", [1, P])

        def prologue(b1, xt):
            loaded, made, xk_ready, zero_kept = (
                sem(n) for n in ("pro_loaded", "pro_made", "pro_xk", "pro_zero_kept"))
            loads = [(xt[:], xT), (k0[:], K0), (xa[:].rearrange("p t f -> p (t f)"), xin), (beta_sb[:], beta),
                     (diag_sb[:], diag),
                     (bias0b[:], bias0.partition_broadcast(P)), (bias2b[:], bias2.partition_broadcast(P)),
                     (gam[:], gamma.partition_broadcast(P)),
                     (wl[:], Wl), (wr[:], Wr), (wh[:], Wh), (wg[:], Wg), (w2[:], W2), (win[:], Win), (wout[:], Wout)]
            with nc.Block(no_gpsimd_drain=True) as block:
                @block.sync
                def _(sp):
                    for dst, src in loads:
                        sp.dma_start(dst, src).then_inc(loaded, 16)
                    sp.wait_ge(loaded, 16 * len(loads))

                @block.gpsimd
                def _(pool):
                    nc.gpsimd.memset(ones[:], 1.0).then_inc(made, 1)
                    pool.wait_ge(made, 1)
                    nc.gpsimd.affine_select(out=ident[:], in_=ones[:], compare_op=ALU.is_equal, fill=0.0, base=0,
                                            pattern=[[-1, P]], channel_multiplier=1).then_inc(made, 1)
                    pool.wait_ge(made, 2)
                    nc.gpsimd.memset(zero_row[:], 0.0).then_inc(made, 1)
                    pool.wait_ge(made, 3)
                    pool.dma_start(h_rows[N:N + 1], zero_row[:]).then_inc(zero_kept, 16)
                    pool.wait_ge(zero_kept, 16)

                @block.tensor
                def _(pe):
                    pe.wait_ge(loaded, 16 * len(loads))
                    for t in range(T):
                        ins = pe.matmul(ps[:, t // 4, (t % 4) * P:(t % 4 + 1) * P], xt[:, t * P:(t + 1) * P], k0[:],
                                        start=True, stop=True)
                        if t % 4 == 3:
                            ins.then_inc(xk_ready, 1)

                @block.vector
                def _(dve):
                    dve.wait_ge(loaded, 16 * len(loads))
                    dve.wait_ge(made, 2)
                    nc.vector.tensor_tensor(off_diag[:], ones[:], ident[:], ALU.subtract)
                    for b in range(T // 4):
                        s = slice(4 * b, 4 * b + 4)
                        nc.vector.tensor_tensor(res[:, s, :], xa[:, s, :],
                                                bias0b[:].unsqueeze(1).broadcast_to((P, 4, P)), ALU.add)
                        dve.wait_ge(xk_ready, b + 1)
                        nc.vector.tensor_tensor(b1[:, s, :], ps[:, b, :].rearrange("p (t f) -> p t f", f=P),
                                                bcast(beta_sb[:, s], P), ALU.mult)

        def aggregate(name, stream, x, right, finish, steps, degree=None, store=None, norm=True, stored_from=None):
            view = stream.rearrange("(m q p) (g w) -> m g p q w", q=Q, p=P, w=GW)
            loaded = [sem(f"{name}_loaded{s}") for s in range(RING)]
            slot_used, agg_copied, y_ready, y_used, v_own = (
                sem(f"{name}_{n}") for n in ("slot_used", "agg_copied", "y_ready", "y_used", "v_own"))
            summed, deg_acc, deg_ready = (
                sem(f"{name}_{n}") if degree is not None else None for n in ("summed", "deg_acc", "deg_ready"))
            done, stored = (sem(f"{name}_{n}") if store is not None else None for n in ("done", "stored"))
            var_ready, std_ready = (sem(f"{name}_{n}") if norm else None for n in ("var_ready", "std_ready"))
            with ExitStack() as own:
                ring = sb(f"{name}_ring", [P, RING, Q, GW], F32, own)
                aggT = sb(f"{name}_aggT", [P, 2, GW], F32, own)
                if degree is not None:
                    pair = sb(f"{name}_pair", [P, 2, GW], F32, own)
                    acc = sb(f"{name}_acc", [P, GW], F32, own)
                y = ps[:, 4:6, :].rearrange("p b (t f) -> p (b t) f", f=P)
                work = sb(f"{name}_work", [P, 2, TG, P], F32, own)
                stats = sb(f"{name}_stats", [P, TG, 6], F32, own)
                mv = sb(f"{name}_mv", [P, TG, 2], F32, own)
                rstd = sb(f"{name}_rstd", [P, TG], F32, own)
                block = own.enter_context(nc.Block(no_gpsimd_drain=True))

                @block.sync
                def _(sp):
                    with sp.Fori(0, G // 2) as it:
                        for h in range(2):
                            for m in range(M):
                                sp.wait_ge(slot_used, (it * 2 + h) * M + m + 1)
                                if degree is not None:
                                    sp.wait_ge(summed, (it * 2 + h) * M + m + 1)
                                sp.dma_start(ring[:, m % RING], view[m, it * 2 + h]).then_inc(loaded[m % RING], 16)

                @block.tensor
                def _(pe):
                    pe.sem_inc(slot_used, RING)
                    with pe.Fori(0, G // 2) as it:
                        for h in range(2):
                            g = it * 2 + h
                            for m in range(M):
                                pe.wait_ge(loaded[m % RING], (g * (M // RING) + m // RING + 1) * 16)
                                if m == 0:
                                    pe.wait_ge(agg_copied, g + 1)
                                for q in range(Q):
                                    c = m * Q + q
                                    for b in range(2):
                                        ins = pe.matmul(ps[:, 2 * h + b, :], x[:, c, :],
                                                        ring[:, m % RING, q, b * BANK:(b + 1) * BANK],
                                                        start=c == 0, stop=c == T - 1)
                                ins.then_inc(slot_used, 1)
                            if degree is not None:
                                pe.wait_ge(deg_acc, g + 1)
                                for k in range(TG):
                                    ins = pe.matmul(ps[:, 6, k:k + 1], acc[:, k * P:(k + 1) * P], ones[:, 0:1],
                                                    start=True, stop=True)
                                ins.then_inc(deg_ready, 1)
                            pe.wait_ge(agg_copied, g + 3)
                            pe.wait_ge(y_used, g + 1)
                            for k in range(TG):
                                ins = pe.matmul(y[:, k, :], aggT[:, h, k * P:(k + 1) * P], right[:],
                                                start=True, stop=True)
                            ins.then_inc(y_ready, 1)

                @block.scalar
                def _(act):
                    act.sem_inc(agg_copied, 2)
                    with act.Fori(0, G // 2) as it:
                        for h in range(2):
                            act.wait_ge(slot_used, (it * 2 + h) * M + M + RING)
                            nc.scalar.copy(aggT[:, h, :], ps[:, 2 * h:2 * h + 2, :].rearrange("p b w -> p (b w)")
                                           ).then_inc(agg_copied, 1)
                            if norm:
                                act.wait_ge(var_ready, it * 2 + h + 1)
                                nc.scalar.activation(rstd[:], rstd[:], ACT.Sqrt).then_inc(std_ready, 1)

                @block.vector
                def _(dve):
                    dve.sem_inc(y_used, 1)
                    summing = 3 * M - 2 + 1 if degree is not None else 0
                    if degree is not None:
                        dve.sem_inc(summed, RING)
                    with dve.Fori(0, G // 2) as it:
                        for h in range(2):
                            g = it * 2 + h
                            own_n = Count(g * (summing + steps))
                            if degree is not None:
                                for m in range(M):
                                    dve.wait_ge(loaded[m % RING], (g * (M // RING) + m // RING + 1) * 16)
                                    r = ring[:, m % RING]
                                    nc.vector.tensor_tensor(pair[:, 0, :], r[:, 0, :], r[:, 1, :], ALU.add
                                                            ).then_inc(v_own, own_n.up())
                                    nc.vector.tensor_tensor(pair[:, 1, :], r[:, 2, :], r[:, 3, :], ALU.add
                                                            ).then_inc(summed, 1)
                                    dve.wait_ge(summed, g * M + m + 1 + RING)
                                    dve.wait_ge(v_own, own_n.now)
                                    if m == 0:
                                        nc.vector.tensor_tensor(acc[:], pair[:, 0, :], pair[:, 1, :], ALU.add
                                                                ).then_inc(v_own, own_n.up())
                                        dve.wait_ge(v_own, own_n.now)
                                        continue
                                    nc.vector.tensor_tensor(pair[:, 0, :], pair[:, 0, :], pair[:, 1, :], ALU.add
                                                            ).then_inc(v_own, own_n.up())
                                    dve.wait_ge(v_own, own_n.now)
                                    last = nc.vector.tensor_tensor(acc[:], acc[:], pair[:, 0, :], ALU.add)
                                    if m < M - 1:
                                        last.then_inc(v_own, own_n.up())
                                        dve.wait_ge(v_own, own_n.now)
                                    else:
                                        last.then_inc(deg_acc, 1)
                                dve.wait_ge(deg_ready, g + 1)
                                nc.vector.tensor_copy(degree[:, bass.ds(g * TG, TG)], ps[:, 6, 0:TG]
                                                      ).then_inc(v_own, own_n.up())
                                dve.wait_ge(v_own, own_n.now)
                                assert own_n.n == summing, (own_n.n, summing)
                            dve.wait_ge(y_ready, g + 1)
                            if store is not None and stored_from is None:
                                dve.wait_ge(stored, g * 16)
                            finish(dve, g, y, y_used, v_own, own_n, work, stats, mv, rstd,
                                   (var_ready, std_ready, g + 1), done)
                            assert own_n.n == summing + steps, (own_n.n, summing, steps)

                if store is not None:
                    rows = store.rearrange("(g t p) f -> g p t f", t=TG, p=P)
                    made = (lambda g: work[:, 1]) if stored_from is None else stored_from

                    @block.gpsimd
                    def _(pool):
                        with pool.Fori(0, G) as g:
                            pool.wait_ge(done, g + 1)
                            pool.dma_start(rows[g], made(g)).then_inc(stored, 16)
                        pool.wait_ge(stored, 16 * G)

        NORM_STEPS = 2 * TG + 3

        def normalize(dve, v_own, own_n, work, stats, mv, rstd, root, to, done=None):
            for k in range(TG):
                nc.vector.bn_stats(stats[:, k, :], work[:, 0, k, :]).then_inc(v_own, own_n.up())
            wait_apart(dve, v_own, own_n.now, passed)
            for k in range(TG):
                nc.vector.bn_aggr(mv[:, k, :], stats[:, k, :]).then_inc(v_own, own_n.up())
            dve.wait_ge(v_own, own_n.now)
            var_ready, std_ready, turn_no = root
            nc.vector.tensor_scalar(rstd[:], mv[:, :, 1], EPS, None, ALU.add).then_inc(var_ready, 1)
            nc.vector.tensor_tensor(work[:, 0], work[:, 0], bcast(mv[:, :, 0], P), ALU.subtract
                                    ).then_inc(v_own, own_n.up())
            dve.wait_ge(std_ready, turn_no)
            nc.vector.reciprocal(rstd[:], rstd[:]).then_inc(v_own, own_n.up())
            dve.wait_ge(v_own, own_n.now)
            last = nc.vector.tensor_tensor(to, work[:, 0], bcast(rstd[:], P), ALU.mult)
            if done is not None:
                last.then_inc(done[0], 1)
                dve.wait_ge(done[0], done[1])
            else:
                last.then_inc(v_own, own_n.up())
                dve.wait_ge(v_own, own_n.now)

        with ExitStack() as own:
            b1 = sb("b1", [P, T, P], F32, own)
            with ExitStack() as inner:
                xt = sb("xt", [P, N], F32, inner)
                prologue(b1, xt)

            inv = sb("inv", [P, TG], F32, own)

            def finish0(dve, g, y, y_used, v_own, n, work, stats, mv, rstd, root, done):
                tiles = bass.ds(g * TG, TG)
                w = work[:, 0]
                nc.vector.tensor_tensor(inv[:], rowdeg[:, tiles], beta_sb[:, tiles], ALU.add).then_inc(v_own, n.up())
                dve.wait_ge(v_own, n.now)
                nc.vector.reciprocal(inv[:], inv[:]).then_inc(v_own, n.up())
                nc.vector.tensor_tensor(w, y, b1[:, tiles, :], ALU.add).then_inc(y_used, 1)
                dve.wait_ge(y_used, g + 2)
                dve.wait_ge(v_own, n.now)
                nc.vector.tensor_tensor(w, w, bcast(inv[:], P), ALU.mult).then_inc(v_own, n.up())
                dve.wait_ge(v_own, n.now)
                nc.vector.tensor_tensor(w, w, res[:, tiles, :], ALU.add).then_inc(v_own, n.up())
                dve.wait_ge(v_own, n.now)
                normalize(dve, v_own, n, work, stats, mv, rstd, root, xb[:, tiles, :])

            aggregate("l0", adjT, xa, k0, finish0, 4 + NORM_STEPS, degree=rowdeg)

        def project(x, HT, HlT, HrT):
            numbered, turned, ht_ready, l_ready, l_copied, r_ready, r_copied = (
                sem(f"proj_{n}") for n in ("numbered", "turned", "ht_ready", "l_ready", "l_copied", "r_ready", "r_copied"))
            with nc.Block(no_gpsimd_drain=True) as block:
                @block.gpsimd
                def _(pool):
                    nc.gpsimd.iota(numbers[:], pattern=[[1, N]], base=1, channel_multiplier=0,
                                   allow_small_or_imprecise_dtypes=True).then_inc(numbered, 1)
                    pool.wait_ge(numbered, 1)

                @block.tensor
                def _(pe):
                    for b in range(8):
                        for k in range(4):
                            ins = pe.matmul(ps[:, b, k * P:(k + 1) * P], x[:, 4 * b + k, :], ident[:],
                                            start=True, stop=True)
                        ins.then_inc(turned, 1)
                    for b in range(8):
                        pe.wait_ge(ht_ready, b + 1)
                        pe.matmul(ps[:, b, :], wl[:], HT[:, b * BANK:(b + 1) * BANK], start=True, stop=True
                                  ).then_inc(l_ready, 1)
                    for b in range(8):
                        pe.wait_ge(l_copied, b + 1)
                        pe.matmul(ps[:, b, :], wr[:], HT[:, b * BANK:(b + 1) * BANK], start=True, stop=True
                                  ).then_inc(r_ready, 1)

                @block.scalar
                def _(act):
                    for b in range(8):
                        act.wait_ge(turned, b + 1)
                        nc.scalar.copy(HT[:, b * BANK:(b + 1) * BANK], ps[:, b, :]).then_inc(ht_ready, 1)
                    for b in range(8):
                        act.wait_ge(r_ready, b + 1)
                        nc.scalar.copy(HrT[:, b * BANK:(b + 1) * BANK], ps[:, b, :]).then_inc(r_copied, 1)

                @block.vector
                def _(dve):
                    for b in range(8):
                        dve.wait_ge(l_ready, b + 1)
                        nc.vector.tensor_copy(HlT[:, b * BANK:(b + 1) * BANK], ps[:, b, :]).then_inc(l_copied, 1)

        class Lister:

            PARTS = 2 + SEG
            STEPS = SEG + 5

            def __init__(self):
                self.loaded, self.masked, self.made, self.cleared, self.added, self.kept, self.found, self.steps = (
                    [sem(f"lists_{n}{s}") for s in range(2)]
                    for n in ("row_loaded", "masked", "keys_made", "cleared", "added", "kept", "found", "list_steps"))

            def place(self, name, own):
                self.row = sb(f"{name}_row", [P, 2, N], F32, own)
                self.junk = sb(f"{name}_junk", [P, N], BF16, own)
                self.sum1 = sb(f"{name}_sum1", [P, 2], F32, own)
                self.cand = sb(f"{name}_cand", [P, 2, SEG * 8], F32, own)
                self.rest = sb(f"{name}_rest", [P, 2, SEG * 8], F32, own)
                self.top = sb(f"{name}_top", [P, 2, S], F32, own)

            def free_slots(self, act, dve):
                for s in range(2):
                    if act is not None:
                        act.sem_inc(self.added[s], 1)
                    if dve is not None:
                        dve.sem_inc(self.found[s], 1)

            def load(self, sp, s, tile, turn):
                sp.wait_ge(self.found[s], turn + 1)
                sp.wait_ge(self.added[s], turn + 1)
                sp.dma_start(self.row[:, s, :], adj_rows[tile]).then_inc(self.loaded[s], 16)

            def make(self, pool, s, turn):
                wait_apart(pool, self.loaded[s], (turn + 1) * 16, passed_pool)
                row = self.row[:, s, :]
                nc.gpsimd.tensor_scalar(row, row, 0.0, -2.0 * N, ALU.is_equal, ALU.mult).then_inc(self.masked[s], 1)
                wait_apart(pool, self.masked[s], turn + 1, passed_pool)
                nc.gpsimd.tensor_tensor(row, row, numbers[:], ALU.add).then_inc(self.made[s], 1)

            def add(self, act, s, tile, turn):
                act.wait_ge(self.cleared[s], turn + 1)
                nc.scalar.activation(self.junk[:], self.row[:, s, :], ACT.Relu, accum_out=self.sum1[:, s:s + 1]
                                     ).then_inc(self.added[s], 1)
                act.wait_ge(self.added[s], turn + 2)
                nc.scalar.copy(keysum[:, bass.ds(tile, 1)], self.sum1[:, s:s + 1]).then_inc(self.kept[s], 1)
                act.wait_ge(self.kept[s], turn + 1)

            def find(self, dve, s, tile, turn, part):
                row, w = self.row[:, s, :], N // SEG
                n = Count(turn * self.STEPS)
                if part == 0:
                    dve.wait_ge(self.made[s], turn + 1)
                    block = row[:, bass.ds(tile * P, P)]
                    nc.vector.tensor_tensor(block, block, off_diag[:], ALU.mult).then_inc(self.cleared[s], 1)
                elif part <= SEG:
                    if part == 1:
                        wait_apart(dve, self.cleared[s], turn + 1, passed)
                    q = part - 1
                    nc.vector.max(self.cand[:, s, 8 * q:8 * q + 8], row[:, q * w:(q + 1) * w]
                                  ).then_inc(self.steps[s], 1)
                else:
                    n.up(SEG)
                    have = self.cand
                    for r in range(0, S, 8):
                        top = self.top[:, s, r:r + 8]
                        wait_apart(dve, self.steps[s], n.now, passed)
                        nc.vector.max(top, have[:, s, :]).then_inc(self.steps[s], n.up())
                        wait_apart(dve, self.steps[s], n.now, passed)
                        if r + 8 < S:
                            nc.vector.match_replace(out=self.rest[:, s, :], in_to_replace=top,
                                                    in_values=have[:, s, :], imm_value=0.0
                                                    ).then_inc(self.steps[s], n.up())
                            have = self.rest
                    assert n.n == self.STEPS
                    nc.vector.tensor_scalar(keys[:, bass.ds(tile, 1), :], self.top[:, s, :].unsqueeze(1), 0.0, None,
                                            ALU.max).then_inc(self.found[s], 1)
                    dve.wait_ge(self.found[s], turn + 2)

        lists = Lister()

        def row_maxima(HlT, HrT, rowmax):
            lt_ready, own_v = sem("rm_lt_ready"), sem("rm_own")
            scored = [sem("rm_scored0"), sem("rm_scored1")]
            taken = [sem("rm_taken0"), sem("rm_taken1")]
            with ExitStack() as own:
                lt = sb("lt", [P, 2, P], F32, own)
                mx = sb("mx", [P, 2, 2], F32, own)
                lists.place("rm", own)
                block = own.enter_context(nc.Block(no_gpsimd_drain=True))

                @block.sync
                def _(sp):
                    with sp.Fori(0, T // 4) as it:
                        for s in range(2):
                            lists.load(sp, s, it * 2 + s, it)

                @block.gpsimd
                def _(pool):
                    with pool.Fori(0, T // 4) as it:
                        for s in range(2):
                            lists.make(pool, s, it)

                @block.scalar
                def _(act):
                    lists.free_slots(act, None)
                    with act.Fori(0, T // 4) as it:
                        for h in range(4):
                            act.wait_ge(scored[1], it * 4 + h + 1)
                            nc.scalar.copy(lt[:, h % 2, :], HlT[:, bass.ds((it * 4 + h) * P, P)]).then_inc(lt_ready, 1)
                            if h >= 2:
                                lists.add(act, h - 2, it * 2 + h - 2, it)

                @block.tensor
                def _(pe):
                    pe.sem_inc(scored[1], 2)
                    with pe.Fori(0, T // 4) as it:
                        for h in range(4):
                            t = it * 4 + h
                            pe.wait_ge(lt_ready, t + 1)
                            for u in range(2):
                                pe.wait_ge(taken[u], t + 1)
                                for b in range(4 * u, 4 * u + 4):
                                    ins = pe.matmul(ps[:, b, :], lt[:, h % 2, :], HrT[:, b * BANK:(b + 1) * BANK],
                                                    start=True, stop=True)
                                ins.then_inc(scored[u], 1)

                @block.vector
                def _(dve):
                    lists.free_slots(None, dve)
                    dve.sem_inc(taken[0], 1)
                    dve.sem_inc(taken[1], 1)
                    with dve.Fori(0, T // 4) as it:
                        for h in range(4):
                            t = it * 4 + h
                            for u in range(2):
                                dve.wait_ge(scored[u], t + 1 + 2 * u)
                                nc.vector.tensor_reduce(mx[:, h % 2, u:u + 1],
                                                        ps[:, 4 * u:4 * u + 4, :].rearrange("p b w -> p (b w)"),
                                                        AX.X, ALU.max).then_inc(taken[u], 1)
                            for u in range(2):
                                dve.wait_ge(taken[u], t + 2)
                            nc.vector.tensor_tensor(rowmax[:, bass.ds(t, 1)], mx[:, h % 2, 0:1], mx[:, h % 2, 1:2], ALU.max
                                                    ).then_inc(own_v, 1)
                            dve.wait_ge(own_v, t + 1)
                            if h % 2 == 0:
                                for part in range(lists.PARTS):
                                    lists.find(dve, h // 2, it * 2 + h // 2, it, part)

        def spread_maxima(rowmax, mb):
            spread, made, copied = sem("sp_spread"), sem("sp_made"), sem("sp_copied")
            with ExitStack() as own:
                diag = sb("diag", [P, 2, 4, P], F32, own)
                block = own.enter_context(nc.Block(no_gpsimd_drain=True))

                @block.vector
                def _(dve):
                    for b in range(8):
                        if b >= 2:
                            dve.wait_ge(spread, b - 1)
                        nc.vector.tensor_tensor(diag[:, b % 2], ident[:].unsqueeze(1).broadcast_to((P, 4, P)),
                                                bcast(rowmax[:, 4 * b:4 * b + 4], P), ALU.mult).then_inc(made, 1)

                @block.tensor
                def _(pe):
                    for b in range(8):
                        pe.wait_ge(made, b + 1)
                        pe.matmul(ps[:, b, :], ones[:], diag[:, b % 2].rearrange("p t f -> p (t f)"),
                                  start=True, stop=True).then_inc(spread, 1)

                @block.scalar
                def _(act):
                    for b in range(8):
                        act.wait_ge(spread, b + 1)
                        nc.scalar.copy(mb[:, b * BANK:(b + 1) * BANK], ps[:, b, :]).then_inc(copied, 1)

        def attend(x, HlT, HrT, mb):
            R = 4
            LAG = 2
            LIST_AT = 3
            st_ready, pt_ready, sum_done, pv_done, s_ready, bt_copied, z_ready, z_copied, o_ready, o_used, own_v = (
                sem(f"at_{n}") for n in ("st_ready", "pt_ready", "sum_done", "pv_done", "s_ready", "bt_copied",
                                         "z_ready", "z_copied", "o_ready", "o_used", "own"))
            with ExitStack() as own:
                st = sb("st", [P, R, BANK], F32, own)
                pt = sb("pt", [P, R, BANK], F32, own)
                sumP = sb("sumP", [P, BANK], F32, own)
                btS = sb("btS", [P, BANK], F32, own)
                zS = sb("zS", [P, BANK], F32, own)
                rl = sb("rl", [P, 4], F32, own)
                w4 = sb("w4", [P, 4, P], F32, own)
                lists.place("at", own)
                block = own.enter_context(nc.Block(no_gpsimd_drain=True))

                @block.sync
                def _(sp):
                    with sp.Fori(0, N // BANK) as ig:
                        for s in range(2):
                            lists.load(sp, s, ig * 2 + s + T // 2, ig + T // 4)

                @block.gpsimd
                def _(pool):
                    with pool.Fori(0, N // BANK) as ig:
                        for s in range(2):
                            lists.make(pool, s, ig + T // 4)

                @block.tensor
                def _(pe):
                    pe.sem_inc(pv_done, R)
                    with pe.Fori(0, N // BANK) as ig:
                        for s in range(T + LAG):
                            if s < T:
                                pe.wait_ge(st_ready, ig * T + s + 1)
                                pe.matmul(ps[:, s % R, :], HrT[:, s * P:(s + 1) * P], HlT[:, bass.ds(ig * BANK, BANK)],
                                          start=True, stop=True).then_inc(s_ready, 1)
                            if s >= LAG:
                                j = s - LAG
                                pe.wait_ge(pt_ready, ig * T + j + 1 + R)
                                if j == 0:
                                    pe.wait_ge(bt_copied, ig + 1)
                                pe.matmul(ps[:, 4, :], x[:, j, :], pt[:, j % R, :], start=j == 0, stop=j == T - 1
                                          ).then_inc(pv_done, 1)
                        pe.wait_ge(bt_copied, ig + 2)
                        pe.matmul(ps[:, 5, :], wh[:], btS[:], start=True, stop=True).then_inc(z_ready, 1)
                        pe.wait_ge(o_used, ig + 1)
                        pe.wait_ge(sum_done, ig * T + T + R)
                        for k in range(4):
                            pe.matmul(ps[:, 7, k:k + 1], sumP[:, k * P:(k + 1) * P], ones[:, 0:1],
                                      start=True, stop=True)
                        pe.wait_ge(z_copied, ig + 1)
                        for k in range(4):
                            ins = pe.matmul(ps[:, 6, k * P:(k + 1) * P], zS[:, k * P:(k + 1) * P], wg[:],
                                            start=True, stop=True)
                        ins.then_inc(o_ready, 1)

                @block.scalar
                def _(act):
                    act.sem_inc(pt_ready, R)
                    act.sem_inc(bt_copied, 1)
                    with act.Fori(0, N // BANK) as ig:
                        for s in range(T):
                            act.wait_ge(st_ready, ig * T + s + 1 + R)
                            act.wait_ge(pv_done, ig * T + s + 1)
                            act.wait_ge(sum_done, ig * T + s + 1)
                            nc.scalar.activation(pt[:, s % R, :], st[:, s % R, :], ACT.Exp).then_inc(pt_ready, 1)
                            if s % (T // 2) == LIST_AT + 3:
                                a = s // (T // 2)
                                lists.add(act, a, ig * 2 + a + T // 2, ig + T // 4)
                        act.wait_ge(pv_done, ig * T + T + R)
                        nc.scalar.copy(btS[:], ps[:, 4, :]).then_inc(bt_copied, 1)
                        act.wait_ge(z_ready, ig + 1)
                        nc.scalar.copy(zS[:], ps[:, 5, :]).then_inc(z_copied, 1)

                @block.vector
                def _(dve):
                    dve.sem_inc(st_ready, R)
                    dve.sem_inc(sum_done, R)
                    dve.sem_inc(o_used, 1)
                    with dve.Fori(0, N // BANK) as ig:
                        for s in range(T + LAG):
                            if s < T:
                                dve.wait_ge(s_ready, ig * T + s + 1)
                                dve.wait_ge(pt_ready, ig * T + s + 1)
                                nc.vector.tensor_tensor(st[:, s % R, :], ps[:, s % R, :],
                                                        mb[:, bass.ds(ig * BANK, BANK)], ALU.subtract
                                                        ).then_inc(st_ready, 1)
                                part = s % (T // 2) - LIST_AT
                                if 0 <= part < lists.PARTS:
                                    a = s // (T // 2)
                                    lists.find(dve, a, ig * 2 + a + T // 2, ig + T // 4, part)
                            if s >= LAG:
                                j = s - LAG
                                dve.wait_ge(pt_ready, ig * T + j + 1 + R)
                                if j == 0:
                                    nc.vector.tensor_copy(sumP[:], pt[:, 0, :]).then_inc(sum_done, 1)
                                else:
                                    dve.wait_ge(sum_done, ig * T + j + R)
                                    nc.vector.tensor_tensor(sumP[:], sumP[:], pt[:, j % R, :], ALU.add
                                                            ).then_inc(sum_done, 1)
                        tiles = bass.ds(ig * 4, 4)
                        dve.wait_ge(o_ready, ig + 1)
                        nc.vector.reciprocal(rl[:], ps[:, 7, 0:4]).then_inc(own_v, 1)
                        dve.wait_ge(own_v, ig * 3 + 1)
                        nc.vector.tensor_scalar(rl[:], rl[:], gam[:, 0:1], None, ALU.mult).then_inc(own_v, 1)
                        dve.wait_ge(own_v, ig * 3 + 2)
                        nc.vector.tensor_tensor(w4[:], ps[:, 6, :].rearrange("p (t f) -> p t f", f=P),
                                                bcast(rl[:], P), ALU.mult).then_inc(o_used, 1)
                        dve.wait_ge(o_used, ig + 2)
                        nc.vector.tensor_tensor(res[:, tiles, :], w4[:], x[:, tiles, :], ALU.add).then_inc(own_v, 1)
                        dve.wait_ge(own_v, ig * 3 + 3)

        with ExitStack() as own:
            HlT = sb("HlT", [P, N], F32, own)
            HrT = sb("HrT", [P, N], F32, own)
            numbers = sb("numbers", [P, N], F32, own)
            with ExitStack() as inner:
                HT = sb("HT", [P, N], F32, inner)
                project(xb, HT, HlT, HrT)
            mb = sb("mb", [P, N], F32, own)
            rowmax = sb("rowmax", [P, T], F32, own)
            row_maxima(HlT, HrT, rowmax)
            spread_maxima(rowmax, mb)
            attend(xb, HlT, HrT, mb)

        def settle_lists():
            own_v, total, small, aux = sem("sl_own"), sem("sl_total"), sem("sl_small"), sem("sl_aux")
            with ExitStack() as own:
                tnum = sb("sl_tnum", [P, T], F32, own)
                f1 = sb("sl_f1", [P, T], F32, own)
                over = sb("sl_over", [P, T], F32, own)
                bad = sb("sl_bad", [P, 3], F32, own)
                spare = sb("sl_spare", [P, T, S], F32, own)
                picked = sb("sl_picked", [P, E, S - K], F32, own)
                sel = sb("sl_sel", [P, S - K, T], F32, own)
                block = own.enter_context(nc.Block(no_gpsimd_drain=True))

                @block.gpsimd
                def _(pool):
                    nc.gpsimd.iota(tnum[:], pattern=[[1, T]], base=1, channel_multiplier=0,
                                   allow_small_or_imprecise_dtypes=True).then_inc(small, 1)
                    pool.wait_ge(small, 1)

                @block.vector
                def _(dve):
                    n = Count()

                    def rows(dst, src, spare):
                        nc.vector.tensor_scalar(spare, src, 0.0, float(N + 1), ALU.is_equal, ALU.mult
                                                ).then_inc(own_v, n.up())
                        dve.wait_ge(own_v, n.now)
                        nc.vector.tensor_tensor(spare, spare, src, ALU.add).then_inc(own_v, n.up())
                        dve.wait_ge(own_v, n.now)
                        nc.vector.tensor_scalar(dst, spare, -1.0, None, ALU.add).then_inc(own_v, n.up())
                        dve.wait_ge(own_v, n.now)

                    nc.vector.tensor_reduce(f1[:], keys[:], AX.X, ALU.add).then_inc(own_v, n.up())
                    dve.wait_ge(own_v, n.now)
                    nc.vector.tensor_tensor(f1[:], f1[:], keysum[:], ALU.not_equal).then_inc(own_v, n.up())
                    dve.wait_ge(own_v, n.now)
                    nc.vector.tensor_reduce(bad[:, 0:1], f1[:], AX.X, ALU.add).then_inc(own_v, n.up())
                    nc.vector.tensor_scalar(over[:], keys[:, :, K], 0.0, None, ALU.is_gt).then_inc(own_v, n.up())
                    dve.wait_ge(own_v, n.now)
                    nc.vector.tensor_reduce(bad[:, 1:2], over[:], AX.X, ALU.add).then_inc(own_v, n.up())
                    dve.wait_ge(small, 1)
                    nc.vector.tensor_tensor(over[:], over[:], tnum[:], ALU.mult).then_inc(own_v, n.up())
                    dve.wait_ge(own_v, n.now)
                    nc.vector.tensor_scalar(bad[:, 1:2], bad[:, 1:2], float(E), None, ALU.is_gt
                                            ).then_inc(own_v, n.up())
                    nc.vector.max(esel[:], over[:]).then_inc(own_v, n.up())
                    dve.wait_ge(own_v, n.now)
                    nc.vector.tensor_tensor(bad[:, 2:3], bad[:, 0:1], bad[:, 1:2], ALU.add).then_inc(aux, 1)
                    nc.vector.tensor_scalar(diag_sb[:], diag_sb[:], 0.0, None, ALU.not_equal
                                            ).then_inc(own_v, n.up())
                    dve.wait_ge(own_v, n.now)
                    nc.vector.tensor_tensor(count[:], diag_sb[:], keys[:, :, 0], ALU.add).then_inc(own_v, n.up())
                    rows(main_idx[:, 0:T, :], keys[:, :, 0:K], spare[:, :, 0:K])
                    nc.vector.memset(main_idx[:, T:T + 2, :], 0)
                    for e in range(E):
                        nc.vector.tensor_scalar(emask[:, e, :], tnum[:], esel[:, e:e + 1], None, ALU.is_equal
                                                ).then_inc(own_v, n.up())
                        dve.wait_ge(own_v, n.now)
                        nc.vector.tensor_tensor(sel[:], keys[:, :, K:S].rearrange("p t k -> p k t"),
                                                emask[:, e, :].unsqueeze(1).broadcast_to((P, S - K, T)), ALU.mult
                                                ).then_inc(own_v, n.up())
                        dve.wait_ge(own_v, n.now)
                        nc.vector.tensor_reduce(picked[:, e, :], sel[:], AX.X, ALU.add).then_inc(own_v, n.up())
                        dve.wait_ge(own_v, n.now)
                    rows(extra_idx[:], picked[:], spare[:, 0:E, 0:S - K])
                    dve.wait_ge(total, 1)
                    nc.vector.tensor_scalar(ok[:], ps[:, 0, 0:1], 0.0, None, ALU.is_equal).then_inc(own_v, n.up())
                    dve.wait_ge(own_v, n.now)

                @block.tensor
                def _(pe):
                    pe.wait_ge(aux, 1)
                    pe.matmul(ps[:, 0, 0:1], ones[:], bad[:, 2:3], start=True, stop=True).then_inc(total, 1)

        settle_lists()

        def finish1(dve, g, y, y_used, v_own, n, work, stats, mv, rstd, root, done):
            tiles = bass.ds(g * TG, TG)
            nc.vector.tensor_tensor(work[:, 0], y, res[:, tiles, :], ALU.add).then_inc(y_used, 1)
            dve.wait_ge(y_used, g + 2)
            normalize(dve, v_own, n, work, stats, mv, rstd, root, xa[:, tiles, :])

        aggregate("l1", adjT, xb, ident, finish1, NORM_STEPS)

        def finish2(dve, g, y, y_used, v_own, n, work, stats, mv, rstd, root, done):
            tiles = bass.ds(g * TG, TG)
            nc.vector.tensor_tensor(work[:, 0], y, bias2b[:].unsqueeze(1).broadcast_to((P, TG, P)), ALU.add
                                    ).then_inc(y_used, 1)
            dve.wait_ge(y_used, g + 2)
            nc.vector.tensor_scalar(res[:, tiles, :], work[:, 0], 0.0, None, ALU.max).then_inc(done, 1)
            dve.wait_ge(done, g + 1)

        aggregate("l2", adjT, xa, w2, finish2, 0, norm=False, store=h_rows[0:N],
                  stored_from=lambda g: res[:, bass.ds(g * TG, TG), :])

        def neighbourhood_maxima():
            staged, gathered, extra_used, extra_in = ([sem(f"nm_{n}{s}") for s in range(2)] for n in
                                                      ("staged", "gathered", "extra_used", "extra_in"))
            row_loaded, spread, taken = ([sem(f"nm_{n}{s}") for s in range(2)] for n in
                                         ("row_loaded", "spread", "taken"))
            own_v, v_own, var_ready, std_ready, turned, turned_kept, made, own_n = (
                sem(f"nm_{n}") for n in ("own", "norm", "var_ready", "std_ready", "turned", "turned_kept", "made",
                                         "max_kept"))
            W = S - K
            with ExitStack() as own:
                R = sb("nm_R", [P, T, P], F32, own)
                RT = R[:].rearrange("p t f -> p (t f)")
                got = sb("nm_got", [P, 2, K, P], F32, own)
                idx = sb("nm_idx", [P, 2, K], U32, own)
                most = sb("nm_most", [P, 2, P], F32, own)
                low = sb("nm_low", [P, T], F32, own)
                work = sb("nm_work", [P, 2, TG, P], F32, own)
                stats = sb("nm_stats", [P, TG, 6], F32, own)
                mv = sb("nm_mv", [P, TG, 2], F32, own)
                rstd = sb("nm_rstd", [P, TG], F32, own)
                hT = sb("nm_hT", [P, N], F32, own)
                a = sb("nm_a", [P, 2, N], F32, own)
                mask = sb("nm_mask", [P, 2, N], BF16, own)
                identb = sb("nm_identb", [P, P], BF16, own)
                junk = sb("nm_junk", [P, 2, N // 2], BF16, own)
                pm = sb("nm_pm", [P, 2], F32, own)
                block = own.enter_context(nc.Block(no_gpsimd_drain=True))

                def gather_listed(pool):
                    for e in range(E):
                        if e >= 2:
                            pool.wait_ge(extra_used[e % 2], e // 2)
                        for k in range(W):
                            pool.indirect_dma_start(got[:, e % 2, k, :], None, h_rows,
                                                    bass.IndirectOffsetOnAxis(extra_idx[:, e, k:k + 1], 0)
                                                    ).then_inc(extra_in[e % 2], 16)
                    with pool.Fori(0, T // 2) as it:
                        for h in range(2):
                            wait_apart(pool, staged[h], it + 1, passed_pool)
                            for k in range(K):
                                pool.indirect_dma_start(got[:, h, k, :], None, h_rows,
                                                        bass.IndirectOffsetOnAxis(idx[:, h, k:k + 1], 0)
                                                        ).then_inc(gathered[h], 16)

                def roots(act):
                    with act.Fori(0, G) as g:
                        act.wait_ge(var_ready, g + 1)
                        nc.scalar.activation(rstd[:], rstd[:], ACT.Sqrt).then_inc(std_ready, 1)

                def maxima_listed(dve):
                    n = Count()
                    nc.vector.tensor_scalar(low[:], count[:], 0.0, LOWEST, ALU.is_equal, ALU.mult
                                            ).then_inc(own_v, n.up())
                    nc.vector.tensor_tensor(R[:], res[:], bcast(diag_sb[:], P), ALU.mult).then_inc(own_v, n.up())
                    dve.wait_ge(own_v, n.now)
                    for e in range(E):
                        s = e % 2
                        dve.wait_ge(extra_in[s], 16 * W * (e // 2 + 1))
                        nc.vector.tensor_reduce(most[:, s, :], got[:, s, 0:W, :].rearrange("p k f -> p f k"),
                                                AX.X, ALU.max).then_inc(extra_used[s], 1)
                        dve.wait_ge(extra_used[s], e // 2 + 1)
                        for t in range(T):
                            nc.vector.scalar_tensor_tensor(out=R[:, t, :], in0=most[:, s, :],
                                                           scalar=emask[:, e, t:t + 1], in1=R[:, t, :],
                                                           op0=ALU.mult, op1=ALU.max).then_inc(own_v, n.up())
                        dve.wait_ge(own_v, n.now)
                    for h in range(2):
                        nc.vector.tensor_copy(idx[:, h, :], main_idx[:, h, :]).then_inc(staged[h], 1)
                    base = n.now
                    with dve.Fori(0, G) as g:
                        m = Count(base + g * 3 * TG)
                        for k in range(TG):
                            h, t, turn = k % 2, g * TG + k, g * (TG // 2) + k // 2
                            dve.wait_ge(gathered[h], (turn + 1) * (16 * K))
                            nc.vector.tensor_reduce(most[:, h, :], got[:, h].rearrange("p k f -> p f k"),
                                                    AX.X, ALU.max).then_inc(own_v, m.up())
                            dve.wait_ge(own_v, m.now)
                            nc.vector.tensor_copy(idx[:, h, :].unsqueeze(1), main_idx[:, bass.ds(t + 2, 1), :]
                                                  ).then_inc(staged[h], 1)
                            tile = R[:, bass.ds(t, 1), :]
                            nc.vector.tensor_tensor(tile, tile, most[:, h, :].unsqueeze(1), ALU.max
                                                    ).then_inc(own_v, m.up())
                            dve.wait_ge(own_v, m.now)
                            nc.vector.tensor_scalar(work[:, 0, k, :].unsqueeze(1), tile, low[:, bass.ds(t, 1)], None,
                                                    ALU.add).then_inc(own_v, m.up())
                        dve.wait_ge(own_v, m.now)
                        q = Count(g * (NORM_STEPS + 1))
                        tiles = bass.ds(g * TG, TG)
                        nc.vector.tensor_tensor(work[:, 0], work[:, 0], xa[:, tiles, :], ALU.add
                                                ).then_inc(v_own, q.up())
                        dve.wait_ge(v_own, q.now)
                        normalize(dve, v_own, q, work, stats, mv, rstd, (var_ready, std_ready, g + 1),
                                  xb[:, tiles, :])

                def load_rows(sp):
                    with sp.Fori(0, T // 2) as it:
                        for h in range(2):
                            sp.wait_ge(made, it * 4 + 2 * h + 1)
                            sp.dma_start(a[:, h, :], adj_rows[it * 2 + h]).then_inc(row_loaded[h], 16)

                def keep_turned(act):
                    for b in range(8):
                        act.wait_ge(turned, b + 1)
                        nc.scalar.copy(hT[:, b * BANK:(b + 1) * BANK], ps[:, b, :]).then_inc(turned_kept, 1)

                def spread_masks(pe):
                    for b in range(8):
                        for k in range(4):
                            ins = pe.matmul(ps[:, b, k * P:(k + 1) * P], res[:, 4 * b + k, :], ident[:],
                                            start=True, stop=True)
                        ins.then_inc(turned, 1)
                    pe.wait_ge(turned_kept, 8)
                    with pe.Fori(0, T // 2) as it:
                        for h in range(2):
                            wait_apart(pe, made, it * 4 + 2 * h + 6, passed_pe)
                            with pe.Fori(0, P) as i:
                                n = (it * 2 + h) * P + i
                                for u in range(2):
                                    pe.wait_ge(taken[u], n + 1)
                                    for b in range(4 * u, 4 * u + 4):
                                        ins = pe.matmul(ps[:, b, :], identb[:, bass.ds(i, 1)].broadcast_to((P, P)),
                                                        mask[:, h, b * BANK:(b + 1) * BANK], start=True, stop=True)
                                    ins.then_inc(spread[u], 1)
                    pe.wait_ge(own_n, N)
                    for b in range(8):
                        for k in range(4):
                            t = 4 * b + k
                            ins = pe.matmul(ps[:, b, k * P:(k + 1) * P], RT[:, t * P:(t + 1) * P], ident[:],
                                            start=True, stop=True)
                        ins.then_inc(turned, 1)

                def maxima_dense(dve):
                    nc.vector.tensor_copy(identb[:], ident[:]).then_inc(made, 1)
                    dve.wait_ge(made, 1)
                    dve.sem_inc(made, 3)
                    dve.sem_inc(taken[0], 1)
                    dve.sem_inc(taken[1], 1)
                    dve.wait_ge(turned_kept, 8)
                    with dve.Fori(0, T // 2) as it:
                        for h in range(2):
                            t = it * 2 + h
                            dve.wait_ge(row_loaded[h], (it + 1) * 16)
                            nc.vector.tensor_scalar(mask[:, h, :], a[:, h, :], 0.0, None, ALU.not_equal
                                                    ).then_inc(made, 1)
                            dve.wait_ge(made, it * 4 + 2 * h + 5)
                            nc.vector.tensor_reduce(count[:, bass.ds(t, 1)], mask[:, h, :], AX.X, ALU.add
                                                    ).then_inc(made, 1)
                            wait_apart(dve, made, it * 4 + 2 * h + 6, passed)
                            with dve.Fori(0, P) as i:
                                n = t * P + i
                                for u in range(2):
                                    wait_apart(dve, spread[u], n + 1, passed)
                                    nc.vector.tensor_tensor_reduce(
                                        out=junk[:, u, :], in0=hT[:, u * (N // 2):(u + 1) * (N // 2)],
                                        in1=ps[:, 4 * u:4 * u + 4, :].rearrange("p b w -> p (b w)"),
                                        scale=1.0, scalar=0.0, op0=ALU.mult, op1=ALU.max,
                                        accum_out=pm[:, u:u + 1]).then_inc(taken[u], 1)
                                dve.wait_ge(taken[0], n + 2)
                                dve.wait_ge(taken[1], n + 2)
                                nc.vector.tensor_tensor(RT[:, bass.ds(n, 1)], pm[:, 0:1], pm[:, 1:2], ALU.max
                                                        ).then_inc(own_n, 1)
                                dve.wait_ge(own_n, n + 1)
                    n = Count()
                    nc.vector.tensor_scalar(low[:], count[:], 0.0, LOWEST, ALU.is_equal, ALU.mult
                                            ).then_inc(own_v, n.up())
                    dve.wait_ge(own_v, n.now)
                    for g in range(G):
                        tiles = slice(g * TG, (g + 1) * TG)
                        dve.wait_ge(turned, 8 + 2 * g + 2)
                        nc.vector.tensor_tensor(work[:, 0],
                                                ps[:, 2 * g:2 * g + 2, :].rearrange("p b (t f) -> p (b t) f", f=P),
                                                bcast(low[:, tiles], P), ALU.add).then_inc(own_v, n.up())
                        dve.wait_ge(own_v, n.now)
                        nc.vector.tensor_tensor(work[:, 0], work[:, 0], xa[:, tiles, :], ALU.add
                                                ).then_inc(own_v, n.up())
                        dve.wait_ge(own_v, n.now)
                        normalize(dve, own_v, n, work, stats, mv, rstd, (var_ready, std_ready, g + 1), xb[:, tiles, :])

                @block.sync
                def _(sp):
                    lists_hold = sp.value_load(ok[0:1, 0:1])
                    with sp.If(lists_hold <= 0):
                        load_rows(sp)

                @block.tensor
                def _(pe):
                    lists_hold = pe.value_load(ok[0:1, 0:1])
                    with pe.If(lists_hold <= 0):
                        spread_masks(pe)

                @block.gpsimd
                def _(pool):
                    lists_hold = pool.value_load(ok[0:1, 0:1])
                    with pool.If(lists_hold > 0):
                        gather_listed(pool)

                @block.scalar
                def _(act):
                    lists_hold = act.value_load(ok[0:1, 0:1])
                    with act.If(lists_hold <= 0):
                        keep_turned(act)
                    roots(act)

                @block.vector
                def _(dve):
                    lists_hold = dve.value_load(ok[0:1, 0:1])
                    with dve.If(lists_hold > 0):
                        maxima_listed(dve)
                    with dve.Else():
                        maxima_dense(dve)

        neighbourhood_maxima()

        SAFE_STEPS = 5

        def inverse_of(dve, deg, inv, spare, v_own, n):
            nc.vector.tensor_scalar(spare[:], deg, 0.0, None, ALU.is_gt).then_inc(v_own, n.up())
            dve.wait_ge(v_own, n.now)
            nc.vector.tensor_tensor(inv[:], deg, spare[:], ALU.mult).then_inc(v_own, n.up())
            nc.vector.tensor_scalar(spare[:], spare[:], -1.0, 1.0, ALU.mult, ALU.add).then_inc(v_own, n.up())
            dve.wait_ge(v_own, n.now)
            nc.vector.tensor_tensor(inv[:], inv[:], spare[:], ALU.add).then_inc(v_own, n.up())
            dve.wait_ge(v_own, n.now)
            nc.vector.reciprocal(inv[:], inv[:]).then_inc(v_own, n.up())
            dve.wait_ge(v_own, n.now)

        with ExitStack() as own:
            inv3 = sb("inv3", [P, TG], F32, own)
            spare = sb("spare3", [P, TG], F32, own)
            coldeg = sb("coldeg", [P, T], F32, own)

            def finish3(dve, g, y, y_used, v_own, n, work, stats, mv, rstd, root, done):
                tiles = bass.ds(g * TG, TG)
                inverse_of(dve, rowdeg[:, tiles], inv3, spare, v_own, n)
                nc.vector.tensor_tensor(work[:, 0], y, bcast(inv3[:], P), ALU.mult).then_inc(y_used, 1)
                dve.wait_ge(y_used, g + 2)
                nc.vector.tensor_tensor(res[:, tiles, :], work[:, 0], xb[:, tiles, :], ALU.add
                                        ).then_inc(v_own, n.up())
                dve.wait_ge(v_own, n.now)

            aggregate("l3in", adjT, xb, win, finish3, SAFE_STEPS + 1, norm=False)

            def finish4(dve, g, y, y_used, v_own, n, work, stats, mv, rstd, root, done):
                tiles = bass.ds(g * TG, TG)
                inverse_of(dve, coldeg[:, tiles], inv3, spare, v_own, n)
                nc.vector.tensor_tensor(work[:, 0], y, bcast(inv3[:], P), ALU.mult).then_inc(y_used, 1)
                dve.wait_ge(y_used, g + 2)
                nc.vector.tensor_tensor(work[:, 0], work[:, 0], res[:, tiles, :], ALU.add
                                        ).then_inc(v_own, n.up())
                dve.wait_ge(v_own, n.now)
                normalize(dve, v_own, n, work, stats, mv, rstd, root, work[:, 1], (done, g + 1))

            aggregate("l3out", adj, xb, wout, finish4, SAFE_STEPS + NORM_STEPS, degree=coldeg, store=out)


def kernel(x, adj, L0_gnn_kernel, L0_gnn_bias, L0_gnn_beta, L1_gnn_W_l, L1_gnn_W_r, L1_gnn_W_h, L1_gnn_W_g,
           L1_gnn_gamma, L2_gnn_weight, L2_gnn_bias, L3_gnn_W_in, L3_gnn_W_out):
    import numpy as np
    import concourse.bacc as bacc
    from concourse.bass_utils import run_bass_kernel_spmd

    x, adj = np.asarray(x), np.asarray(adj)
    N, D = x.shape
    tiled = x.reshape(N // P, P, D).transpose(1, 0, 2).reshape(P, -1)
    ins = {
        "adj": adj, "adjT": adj.T, "xin": tiled, "xT": x.T, "K0": L0_gnn_kernel,
        "bias0": np.asarray(L0_gnn_bias), "beta": np.asarray(L0_gnn_beta).reshape(N // P, P).T,
        "Wl": L1_gnn_W_l, "Wr": L1_gnn_W_r, "Wh": L1_gnn_W_h, "Wg": L1_gnn_W_g, "gamma": L1_gnn_gamma,
        "diag": np.diagonal(adj).reshape(N // P, P).T,
        "W2": L2_gnn_weight, "bias2": L2_gnn_bias, "Win": L3_gnn_W_in, "Wout": L3_gnn_W_out,
    }
    nc = bacc.Bacc("TRN2", target_bir_lowering=False, num_devices=1)
    arrays, args = {}, {}
    for name, a in ins.items():
        a = np.ascontiguousarray(a)
        arrays[f"in_{name}"] = a
        args[name] = nc.dram_tensor(f"in_{name}", a.shape, mybir.dt.from_np(a.dtype), kind="ExternalInput").ap()
    out = nc.dram_tensor("out_x", (N, D), F32, kind="ExternalOutput").ap()
    build(nc, out=out, **args)
    r = run_bass_kernel_spmd(nc, [arrays], core_ids=[0])
    return r.results[0]["out_x"]
```

```python
from contextlib import ExitStack

import concourse.bass as bass
from concourse import mybir

F32 = mybir.dt.float32
BF16 = mybir.dt.bfloat16
U32 = mybir.dt.uint32
ALU = mybir.AluOpType
ACT = mybir.ActivationFunctionType
AX = mybir.AxisListType

P = 128
BANK = 512
EPS = 1e-5
LOWEST = -3.4028234663852886e38


def bcast(ap, n):
    return ap.unsqueeze(2).broadcast_to((ap.shape[0], ap.shape[1], n))


def wait_apart(eng, sem, value, passed):
    eng.wait_ge(sem, value)
    eng.sem_inc(passed, 1)


class Count:

    def __init__(self, base=0):
        self.base, self.n = base, 0

    def up(self, k=1):
        self.n += k
        return k

    @property
    def now(self):
        return self.base + self.n


def build(nc, adj, adjT, xin, xT, K0, bias0, beta, Wl, Wr, Wh, Wg, gamma, W2, bias2, Win, Wout, diag, out):
    N = adj.shape[0]
    T = N // P
    GW = 2 * BANK
    G = N // GW
    TG = GW // P
    Q = 2
    M = T // Q
    RING = 8
    SEG = 8
    S = 24
    K = 13
    TIERS = ((K, 16, 6), (16, 20, 6), (20, S, 2))
    W = 4
    assert all(to - start <= W and room <= 8 for start, to, room in TIERS) and TIERS[-1][1] == S
    LISTS = sorted(((i, r) for i, (_, _, room) in enumerate(TIERS) for r in range(room)),
                   key=lambda ir: (ir[1] // 2, ir))
    EXTRA = [TIERS[i][1] - TIERS[i][0] for i, _ in LISTS]
    E = len(LISTS)
    STAGES = [[e for e, (_, r) in enumerate(LISTS) if r // 2 == p] for p in range(max(r for _, r in LISTS) // 2 + 1)]
    assert STAGES[0][:1] == [0] and len(STAGES) < 8

    with ExitStack() as ctx:
        def sb(name, shape, dt=F32, stack=ctx):
            return stack.enter_context(nc.sbuf_tensor(name, shape, dt))

        def sem(name):
            return ctx.enter_context(nc.semaphore(name))

        ps = ctx.enter_context(nc.psum_tensor("ps", [P, 8, BANK], F32))

        passed, passed_pool, passed_pe = sem("passed"), sem("passed_pool"), sem("passed_pe")
        adj_rows = adj.rearrange("(t p) j -> t p j", p=P)
        xa = sb("xa", [P, T, P])
        xb = sb("xb", [P, T, P])
        res = sb("res", [P, T, P])
        ident = sb("ident", [P, P])
        ones = sb("ones", [P, P])
        off_diag = sb("off_diag", [P, P])
        k0 = sb("k0", [P, P])
        wl = sb("wl", [P, P])
        wr = sb("wr", [P, P])
        wh = sb("wh", [P, P])
        wg = sb("wg", [P, P])
        w2 = sb("w2", [P, P])
        win = sb("win", [P, P])
        wout = sb("wout", [P, P])
        bias0b = sb("bias0b", [P, P])
        bias2b = sb("bias2b", [P, P])
        gam = sb("gam", [P, 1])
        beta_sb = sb("beta_sb", [P, T])
        rowdeg = sb("rowdeg", [P, T])
        colpart = sb("colpart", [P, G * T])
        count = sb("count", [P, T])
        diag_sb = sb("diag_sb", [P, T])
        keys = sb("keys", [P, T, S])
        keysum = sb("keysum", [P, T, 2])
        tnum = sb("tnum", [P, T])
        main_idx = sb("main_idx", [P, T + 2, K], U32)
        extra_idx = sb("extra_idx", [P, E, W], U32)
        emask = sb("emask", [P, E, T])
        ok = sb("ok", [P, 1], mybir.dt.int32)
        h_rows = nc.dram_tensor("h_rows", [N + 1, P], F32, kind="Internal").ap()

        zero_row = sb("zero_row", [1, P])

        loaded, loaded_first = sem("pro_loaded"), sem("pro_loaded_first")
        loads = [(xa[:].rearrange("p t f -> p (t f)"), xin), (bias0b[:], bias0.partition_broadcast(P)),
                 (diag_sb[:], diag), (bias2b[:], bias2.partition_broadcast(P)),
                 (gam[:], gamma.partition_broadcast(P)),
                 (wl[:], Wl), (wr[:], Wr), (wh[:], Wh), (wg[:], Wg), (w2[:], W2), (win[:], Win), (wout[:], Wout)]

        def prologue(b1, xt):
            made, xk_ready, zero_kept = (sem(n) for n in ("pro_made", "pro_xk", "pro_zero_kept"))
            with nc.Block(no_gpsimd_drain=True) as block:
                @block.sync
                def _(sp):
                    for dst, src in ((xt[:], xT), (k0[:], K0), (beta_sb[:], beta)):
                        sp.dma_start(dst, src).then_inc(loaded_first, 16)
                    for dst, src in loads:
                        sp.dma_start(dst, src).then_inc(loaded, 16)

                @block.gpsimd
                def _(pool):
                    nc.gpsimd.memset(ones[:], 1.0).then_inc(made, 1)
                    pool.wait_ge(made, 1)
                    nc.gpsimd.affine_select(out=ident[:], in_=ones[:], compare_op=ALU.is_equal, fill=0.0, base=0,
                                            pattern=[[-1, P]], channel_multiplier=1).then_inc(made, 1)
                    pool.wait_ge(made, 2)
                    nc.gpsimd.memset(zero_row[:], 0.0).then_inc(made, 1)
                    pool.wait_ge(made, 3)
                    pool.dma_start(h_rows[N:N + 1], zero_row[:]).then_inc(zero_kept, 16)
                    nc.gpsimd.iota(tnum[:], pattern=[[-1, T]], base=T, channel_multiplier=0,
                                   allow_small_or_imprecise_dtypes=True).then_inc(made, 1)
                    pool.wait_ge(made, 4)
                    pool.wait_ge(zero_kept, 16)

                @block.tensor
                def _(pe):
                    pe.wait_ge(loaded_first, 16 * 3)
                    for t in range(T):
                        ins = pe.matmul(ps[:, t // 4, (t % 4) * P:(t % 4 + 1) * P], xt[:, t * P:(t + 1) * P], k0[:],
                                        start=True, stop=True)
                        if t % 4 == 3:
                            ins.then_inc(xk_ready, 1)

                @block.vector
                def _(dve):
                    dve.wait_ge(loaded_first, 16 * 3)
                    dve.wait_ge(made, 2)
                    nc.vector.tensor_tensor(off_diag[:], ones[:], ident[:], ALU.subtract)
                    for b in range(T // 4):
                        s = slice(4 * b, 4 * b + 4)
                        dve.wait_ge(xk_ready, b + 1)
                        nc.vector.tensor_tensor(b1[:, s, :], ps[:, b, :].rearrange("p (t f) -> p t f", f=P),
                                                bcast(beta_sb[:, s], P), ALU.mult)

        class Layer:

            def __init__(self, x, right, finish, steps, norm=True, degree=None, part_sums=None, store=None,
                         pe_first=None, dve_first=None, pe_last=None, dve_last=None):
                self.x, self.right, self.finish, self.steps, self.norm = x, right, finish, steps, norm
                self.degree, self.part_sums, self.store = degree, part_sums, store
                self.pe_first, self.dve_first, self.pe_last, self.dve_last = pe_first, dve_first, pe_last, dve_last

        def aggregate(name, layers):
            view = adjT.rearrange("(m q p) (g w) -> m g p q w", q=Q, p=P, w=GW)
            degree = any(layer.degree is not None for layer in layers)
            part_sums = any(layer.part_sums is not None for layer in layers)
            store = any(layer.store is not None for layer in layers)
            loaded = [sem(f"{name}_loaded{s}") for s in range(RING)]
            slot_used, agg_copied, y_ready, y_used, v_own, group_ready = (
                sem(f"{name}_{n}") for n in ("slot_used", "agg_copied", "y_ready", "y_used", "v_own", "group_ready"))
            summed, deg_acc, deg_ready = (
                sem(f"{name}_{n}") if degree else None for n in ("summed", "deg_acc", "deg_ready"))
            done, stored = (sem(f"{name}_{n}") if store else None for n in ("done", "stored"))
            row_summed = sem(f"{name}_row_summed") if part_sums else None
            var_ready, std_ready = (sem(f"{name}_{n}") for n in ("var_ready", "std_ready"))
            with ExitStack() as own:
                ring = sb(f"{name}_ring", [P, RING, Q, GW], F32, own)
                aggT = sb(f"{name}_aggT", [P, 2, GW], F32, own)
                if part_sums:
                    junk = sb(f"{name}_junk", [P, Q, GW], BF16, own)
                if degree:
                    pair = sb(f"{name}_pair", [P, 2, GW], F32, own)
                    acc = sb(f"{name}_acc", [P, GW], F32, own)
                y = ps[:, 4:6, :].rearrange("p b (t f) -> p (b t) f", f=P)
                work = sb(f"{name}_work", [P, 1, TG, P], F32, own)
                stats = sb(f"{name}_stats", [P, TG, 6], F32, own)
                mv = sb(f"{name}_mv", [P, TG, 2], F32, own)
                rstd = sb(f"{name}_rstd", [P, TG], F32, own)
                block = own.enter_context(nc.Block(no_gpsimd_drain=True))

                def await_load(eng, turn, m):
                    eng.wait_ge(loaded[m % RING], (turn * (M // RING) + m // RING + 1) * 16)

                @block.sync
                def _(sp):
                    for i, layer in enumerate(layers):
                        with sp.Fori(0, G // 2) as it:
                            for h in range(2):
                                for m in range(M):
                                    last_use = (i * G + it * 2 + h) * M + m + 1
                                    sp.wait_ge(slot_used, last_use)
                                    if layer.degree is not None:
                                        sp.wait_ge(summed, last_use)
                                    if layer.part_sums is not None:
                                        sp.wait_ge(row_summed, last_use)
                                    sp.dma_start(ring[:, m % RING], view[m, it * 2 + h]).then_inc(loaded[m % RING], 16)

                @block.tensor
                def _(pe):
                    def group(layer, i, turn, h, m):
                        await_load(pe, turn, m)
                        if m == 0:
                            pe.wait_ge(agg_copied, turn + 1)
                        if i > 0 and m * Q % TG == 0:
                            pe.wait_ge(group_ready, (i - 1) * G + m * Q // TG + 1)
                        for q in range(Q):
                            c = m * Q + q
                            for b in range(2):
                                ins = pe.matmul(ps[:, 2 * h + b, :], layer.x[:, c, :],
                                                ring[:, m % RING, q, b * BANK:(b + 1) * BANK],
                                                start=c == 0, stop=c == T - 1)
                        ins.then_inc(slot_used, 1)

                    def project_group(layer, g, turn, h):
                        if layer.degree is not None:
                            pe.wait_ge(deg_acc, g + 1)
                            for k in range(TG):
                                ins = pe.matmul(ps[:, 6, k:k + 1], acc[:, k * P:(k + 1) * P], ones[:, 0:1],
                                                start=True, stop=True)
                            ins.then_inc(deg_ready, 1)
                        pe.wait_ge(agg_copied, turn + 3)
                        pe.wait_ge(y_used, turn + 1)
                        for k in range(TG):
                            ins = pe.matmul(y[:, k, :], aggT[:, h, k * P:(k + 1) * P], layer.right[:],
                                            start=True, stop=True)
                        ins.then_inc(y_ready, 1)

                    pe.sem_inc(slot_used, RING)
                    for i, layer in enumerate(layers):
                        if layer.pe_first is not None:
                            layer.pe_first(pe)
                        with pe.Fori(0, G // 2) as it:
                            for h in range(2):
                                for m in range(M):
                                    group(layer, i, i * G + it * 2 + h, h, m)
                                    if h == 1 and m == 0:
                                        project_group(layer, it * 2, i * G + it * 2, 0)
                            project_group(layer, it * 2 + 1, i * G + it * 2 + 1, 1)
                        if layer.pe_last is not None:
                            layer.pe_last(pe)

                @block.scalar
                def _(act):
                    def sum_rows(layer, g, turn, m):
                        await_load(act, turn, m)
                        act.wait_ge(row_summed, turn * M + m + RING)
                        for q in range(Q):
                            ins = nc.scalar.activation(junk[:, q, :], ring[:, m % RING, q, :], ACT.Copy,
                                                       accum_out=layer.part_sums[:, bass.ds(g * T + m * Q + q, 1)])
                        ins.then_inc(row_summed, 1)

                    act.sem_inc(agg_copied, 2)
                    for i, layer in enumerate(layers):
                        if layer.part_sums is not None:
                            act.sem_inc(row_summed, i * G * M + RING)
                    for i, layer in enumerate(layers):
                        normed = sum(G for before in layers[:i] if before.norm)
                        with act.Fori(0, G // 2) as it:
                            for h in range(2):
                                g, turn = it * 2 + h, i * G + it * 2 + h
                                if layer.part_sums is not None:
                                    for m in range(M - 1):
                                        sum_rows(layer, g, turn, m)
                                act.wait_ge(slot_used, turn * M + M + RING)
                                nc.scalar.copy(aggT[:, h, :], ps[:, 2 * h:2 * h + 2, :].rearrange("p b w -> p (b w)")
                                               ).then_inc(agg_copied, 1)
                                if layer.part_sums is not None:
                                    sum_rows(layer, g, turn, M - 1)
                                if layer.norm:
                                    act.wait_ge(var_ready, normed + g + 1)
                                    nc.scalar.activation(rstd[:], rstd[:], ACT.Sqrt).then_inc(std_ready, 1)

                @block.vector
                def _(dve):
                    def sum_columns(layer, g, turn, own_n):
                        for m in range(M):
                            await_load(dve, turn, m)
                            r = ring[:, m % RING]
                            if m == 0:
                                nc.vector.tensor_tensor(acc[:], r[:, 0, :], r[:, 1, :], ALU.add).then_inc(summed, 1)
                                dve.wait_ge(summed, turn * M + m + 1 + RING)
                                continue
                            two = pair[:, m % 2, :]
                            nc.vector.tensor_tensor(two, r[:, 0, :], r[:, 1, :], ALU.add).then_inc(summed, 1)
                            dve.wait_ge(summed, turn * M + m + 1 + RING)
                            if m > 1:
                                dve.wait_ge(v_own, own_n.now)
                            last = nc.vector.tensor_tensor(acc[:], acc[:], two, ALU.add)
                            if m < M - 1:
                                last.then_inc(v_own, own_n.up())
                            else:
                                last.then_inc(deg_acc, 1)
                        dve.wait_ge(deg_ready, g + 1)
                        nc.vector.tensor_copy(layer.degree[:, bass.ds(g * TG, TG)], ps[:, 6, 0:TG]
                                              ).then_inc(v_own, own_n.up())
                        dve.wait_ge(v_own, own_n.now)

                    dve.sem_inc(y_used, 1)
                    for i, layer in enumerate(layers):
                        if layer.degree is not None:
                            dve.sem_inc(summed, i * G * M + RING)
                    own_before = normed = 0
                    for i, layer in enumerate(layers):
                        if layer.dve_first is not None:
                            layer.dve_first(dve)
                        steps = layer.steps + (M - 1 if layer.degree is not None else 0)
                        with dve.Fori(0, G // 2) as it:
                            for h in range(2):
                                g, turn = it * 2 + h, i * G + it * 2 + h
                                own_n = Count(own_before + g * steps)
                                if layer.degree is not None:
                                    sum_columns(layer, g, turn, own_n)
                                dve.wait_ge(y_ready, turn + 1)
                                layer.finish(dve, g, turn, y, y_used, v_own, own_n, work, stats, mv, rstd,
                                             (var_ready, std_ready, normed + g + 1), done)
                                assert own_n.n == steps, (own_n.n, steps)
                                if i < len(layers) - 1:
                                    dve.sem_inc(group_ready, 1)
                        own_before += G * steps
                        normed += G if layer.norm else 0
                        if layer.dve_last is not None:
                            layer.dve_last(dve)

                if store:
                    @block.gpsimd
                    def _(pool):
                        for layer in layers:
                            if layer.store is not None:
                                rows = layer.store[0].rearrange("(g t p) f -> g p t f", t=TG, p=P)
                                with pool.Fori(0, G) as g:
                                    pool.wait_ge(done, g + 1)
                                    pool.dma_start(rows[g], layer.store[1][:, bass.ds(g * TG, TG), :]
                                                   ).then_inc(stored, 16)
                                pool.wait_ge(stored, 16 * G)

        NORM_STEPS = 2 * TG + 3

        def normalize(dve, v_own, own_n, work, stats, mv, rstd, root, to, done=None):
            for k in range(stats.shape[1]):
                nc.vector.bn_stats(stats[:, k, :], work[:, 0, k, :]).then_inc(v_own, own_n.up())
            wait_apart(dve, v_own, own_n.now, passed)
            for k in range(stats.shape[1]):
                nc.vector.bn_aggr(mv[:, k, :], stats[:, k, :]).then_inc(v_own, own_n.up())
            dve.wait_ge(v_own, own_n.now)
            var_ready, std_ready, turn_no = root
            nc.vector.tensor_scalar(rstd[:], mv[:, :, 1], EPS, None, ALU.add).then_inc(var_ready, 1)
            nc.vector.tensor_tensor(work[:, 0], work[:, 0], bcast(mv[:, :, 0], P), ALU.subtract
                                    ).then_inc(v_own, own_n.up())
            dve.wait_ge(std_ready, turn_no)
            nc.vector.reciprocal(rstd[:], rstd[:]).then_inc(v_own, own_n.up())
            dve.wait_ge(v_own, own_n.now)
            last = nc.vector.tensor_tensor(to, work[:, 0], bcast(rstd[:], P), ALU.mult)
            if done is not None:
                last.then_inc(done[0], 1)
                dve.wait_ge(done[0], done[1])
            else:
                last.then_inc(v_own, own_n.up())
                dve.wait_ge(v_own, own_n.now)

        with ExitStack() as own:
            b1 = sb("b1", [P, T, P], F32, own)
            with ExitStack() as inner:
                xt = sb("xt", [P, N], F32, inner)
                prologue(b1, xt)

            inv = sb("inv", [P, TG], F32, own)

            def finish0(dve, g, turn, y, y_used, v_own, n, work, stats, mv, rstd, root, done):
                tiles = bass.ds(g * TG, TG)
                w = work[:, 0]
                nc.vector.tensor_tensor(inv[:], rowdeg[:, tiles], beta_sb[:, tiles], ALU.add).then_inc(v_own, n.up())
                dve.wait_ge(v_own, n.now)
                nc.vector.reciprocal(inv[:], inv[:]).then_inc(v_own, n.up())
                nc.vector.tensor_tensor(w, y, b1[:, tiles, :], ALU.add).then_inc(y_used, 1)
                dve.wait_ge(y_used, turn + 2)
                dve.wait_ge(v_own, n.now)
                nc.vector.tensor_tensor(w, w, bcast(inv[:], P), ALU.mult).then_inc(v_own, n.up())
                dve.wait_ge(v_own, n.now)
                nc.vector.tensor_tensor(w, w, res[:, tiles, :], ALU.add).then_inc(v_own, n.up())
                dve.wait_ge(v_own, n.now)
                normalize(dve, v_own, n, work, stats, mv, rstd, root, xb[:, tiles, :])

            def await_loads(eng):
                eng.wait_ge(loaded, 16 * len(loads))

            def add_bias(dve):
                added = sem("bias_added")
                await_loads(dve)
                nc.vector.tensor_tensor(res[:], xa[:], bias0b[:].unsqueeze(1).broadcast_to((P, T, P)), ALU.add
                                        ).then_inc(added, 1)
                dve.wait_ge(added, 1)

            aggregate("l0", [Layer(xa, k0, finish0, 4 + NORM_STEPS, degree=rowdeg, pe_first=await_loads,
                                   dve_first=add_bias)])

        def project(x, HT, HlT, HrT):
            numbered, turned, ht_ready, l_ready, l_copied, r_ready, r_copied = (
                sem(f"proj_{n}") for n in ("numbered", "turned", "ht_ready", "l_ready", "l_copied", "r_ready",
                                           "r_copied"))
            with nc.Block(no_gpsimd_drain=True) as block:
                @block.gpsimd
                def _(pool):
                    nc.gpsimd.iota(numbers[:], pattern=[[1, N]], base=1, channel_multiplier=0,
                                   allow_small_or_imprecise_dtypes=True).then_inc(numbered, 1)
                    pool.wait_ge(numbered, 1)

                @block.tensor
                def _(pe):
                    for b in range(8):
                        for k in range(4):
                            ins = pe.matmul(ps[:, b, k * P:(k + 1) * P], x[:, 4 * b + k, :], ident[:],
                                            start=True, stop=True)
                        ins.then_inc(turned, 1)
                    for b in range(8):
                        pe.wait_ge(ht_ready, b + 1)
                        pe.matmul(ps[:, b, :], wl[:], HT[:, b * BANK:(b + 1) * BANK], start=True, stop=True
                                  ).then_inc(l_ready, 1)
                    for b in range(8):
                        pe.wait_ge(l_copied, b + 1)
                        pe.matmul(ps[:, b, :], wr[:], HT[:, b * BANK:(b + 1) * BANK], start=True, stop=True
                                  ).then_inc(r_ready, 1)

                @block.scalar
                def _(act):
                    for b in range(8):
                        act.wait_ge(turned, b + 1)
                        nc.scalar.copy(HT[:, b * BANK:(b + 1) * BANK], ps[:, b, :]).then_inc(ht_ready, 1)
                    for b in range(8):
                        act.wait_ge(r_ready, b + 1)
                        nc.scalar.copy(HrT[:, b * BANK:(b + 1) * BANK], ps[:, b, :]).then_inc(r_copied, 1)

                @block.vector
                def _(dve):
                    for b in range(8):
                        dve.wait_ge(l_ready, b + 1)
                        nc.vector.tensor_copy(HlT[:, b * BANK:(b + 1) * BANK], ps[:, b, :]).then_inc(l_copied, 1)

        class Lister:

            SLOTS = 3
            PARTS = SEG + 2 * (S // 8)
            STEPS = SEG + 2 * (S // 8) - 1

            def __init__(self):
                self.loaded, self.signed, self.made, self.added, self.kept, self.found, self.steps = (
                    [sem(f"lists_{n}{s}") for s in range(self.SLOTS)]
                    for n in ("row_loaded", "signed", "keys_made", "added", "kept", "found", "list_steps"))

            def place(self, name, own):
                self.row = sb(f"{name}_row", [P, self.SLOTS, N], F32, own)
                self.sum1 = sb(f"{name}_sum1", [P, self.SLOTS, 2], F32, own)
                self.cand = sb(f"{name}_cand", [P, self.SLOTS, SEG * 8], F32, own)
                self.rest = sb(f"{name}_rest", [P, self.SLOTS, SEG * 8], F32, own)
                self.top = sb(f"{name}_top", [P, self.SLOTS, S], F32, own)

            def free_slots(self, dve):
                for s in range(self.SLOTS):
                    dve.sem_inc(self.found[s], 1)

            def load(self, sp, s, tile, turn):
                sp.wait_ge(self.found[s], turn + 1)
                sp.dma_start(self.row[:, s, :], adj_rows[tile]).then_inc(self.loaded[s], 16)

            def half(self, s, part):
                return self.row[:, s, part * (N // 2):(part + 1) * (N // 2)]

            def sign(self, act, s, turn, part):
                act.wait_ge(self.loaded[s], (turn + 1) * 16)
                nc.scalar.activation(self.half(s, part), self.half(s, part), ACT.Sign).then_inc(self.signed[s], 1)

            def number(self, pool, s, tile, turn, part):
                wait_apart(pool, self.signed[s], turn * 2 + part + 1, passed_pool)
                nc.gpsimd.tensor_tensor(self.half(s, part), self.half(s, part),
                                        numbers[:, part * (N // 2):(part + 1) * (N // 2)], ALU.mult
                                        ).then_inc(self.made[s], 1)
                if part == 1:
                    block = self.row[:, s, bass.ds(tile * P, P)]
                    wait_apart(pool, self.made[s], turn * 3 + 2, passed_pool)
                    nc.gpsimd.tensor_tensor(block, block, off_diag[:], ALU.mult).then_inc(self.made[s], 1)

            def add(self, act, s, tile, turn, part):
                act.wait_ge(self.made[s], turn * 3 + 3)
                nc.scalar.activation(self.half(s, part), self.half(s, part), ACT.Abs,
                                     accum_out=self.sum1[:, s, part:part + 1]).then_inc(self.added[s], 1)
                if part == 1:
                    act.wait_ge(self.added[s], turn * 2 + 2)
                    nc.scalar.copy(keysum[:, bass.ds(tile, 1), :], self.sum1[:, s, :].unsqueeze(1)
                                   ).then_inc(self.kept[s], 1)
                    act.wait_ge(self.kept[s], turn + 1)

            def find(self, dve, s, tile, turn, parts):
                row, w = self.row[:, s, :], N // SEG
                dve.sem_inc(passed, 1)
                for part in parts:
                    done = turn * self.STEPS + part
                    if part < SEG:
                        if part == 0:
                            wait_apart(dve, self.added[s], turn * 2 + 2, passed)
                        nc.vector.max(self.cand[:, s, 8 * part:8 * part + 8], row[:, part * w:(part + 1) * w]
                                      ).then_inc(self.steps[s], 1)
                        continue
                    r, replace = (part - SEG) // 2 * 8, (part - SEG) % 2
                    top, have = self.top[:, s, r:r + 8], (self.rest if r else self.cand)[:, s, :]
                    if not replace:
                        wait_apart(dve, self.steps[s], done, passed)
                        nc.vector.max(top, have).then_inc(self.steps[s], 1)
                    elif r + 8 < S:
                        wait_apart(dve, self.steps[s], done, passed)
                        nc.vector.match_replace(out=self.rest[:, s, :], in_to_replace=top, in_values=have,
                                                imm_value=0.0).then_inc(self.steps[s], 1)
                    else:
                        dve.wait_ge(self.steps[s], done)
                        nc.vector.tensor_copy(keys[:, bass.ds(tile, 1), :], self.top[:, s, :].unsqueeze(1)
                                              ).then_inc(self.found[s], 1)
                        dve.wait_ge(self.found[s], turn + 2)

        lists = Lister()
        EARLY = T // 4

        def row_maxima(HlT, HrT, halfmax):
            lt_ready = sem("rm_lt_ready")
            scored = [sem("rm_scored0"), sem("rm_scored1")]
            taken = [sem("rm_taken0"), sem("rm_taken1")]
            with ExitStack() as own:
                lt = sb("lt", [P, 2, P], F32, own)
                lists.place("rm", own)
                block = own.enter_context(nc.Block(no_gpsimd_drain=True))

                U = 8
                SIGN, ADD = (0, 2), (2, 4)
                FIND = (4, 10)
                cuts = (0, 2, 4, 6, 8, 11, lists.PARTS)

                @block.sync
                def _(sp):
                    with sp.Fori(0, T // U) as it:
                        for s in range(2):
                            lists.load(sp, s, it * 2 + s, it)

                @block.gpsimd
                def _(pool):
                    with pool.Fori(0, T // U) as it:
                        for s in range(2):
                            for part in range(2):
                                lists.number(pool, s, it * 2 + s, it, part)

                @block.scalar
                def _(act):
                    with act.Fori(0, T // U) as it:
                        for h in range(U):
                            act.wait_ge(scored[1], it * U + h + 1)
                            nc.scalar.copy(lt[:, h % 2, :], HlT[:, bass.ds((it * U + h) * P, P)]).then_inc(lt_ready, 1)
                            for s in range(2):
                                for part in range(2):
                                    if h == ADD[s]:
                                        lists.add(act, s, it * 2 + s, it, part)
                                for part in range(2):
                                    if h == SIGN[s]:
                                        lists.sign(act, s, it, part)

                @block.tensor
                def _(pe):
                    pe.sem_inc(scored[1], 2)
                    with pe.Fori(0, T // U) as it:
                        for h in range(U):
                            t = it * U + h
                            pe.wait_ge(lt_ready, t + 1)
                            for u in range(2):
                                pe.wait_ge(taken[u], t + 1)
                                for b in range(4 * u, 4 * u + 4):
                                    ins = pe.matmul(ps[:, b, :], lt[:, h % 2, :], HrT[:, b * BANK:(b + 1) * BANK],
                                                    start=True, stop=True)
                                ins.then_inc(scored[u], 1)

                @block.vector
                def _(dve):
                    lists.free_slots(dve)
                    dve.sem_inc(taken[0], 1)
                    dve.sem_inc(taken[1], 1)
                    with dve.Fori(0, T // U) as it:
                        for h in range(U):
                            t = it * U + h
                            for u in range(2):
                                dve.wait_ge(scored[u], t + 1 + 2 * u)
                                nc.vector.tensor_reduce(halfmax[:, bass.ds(t * 2 + u, 1)],
                                                        ps[:, 4 * u:4 * u + 4, :].rearrange("p b w -> p (b w)"),
                                                        AX.X, ALU.max).then_inc(taken[u], 1)
                                for s in range(2):
                                    k = 2 * h + u - FIND[s]
                                    if 0 <= k < len(cuts) - 1:
                                        lists.find(dve, s, it * 2 + s, it, range(cuts[k], cuts[k + 1]))

        def spread_maxima(halfmax, mb):
            spread, made, copied, joined = (sem(f"sp_{n}") for n in ("spread", "made", "copied", "joined"))
            with ExitStack() as own:
                rowmax = sb("rowmax", [P, T], F32, own)
                diag = sb("diag", [P, 2, 4, P], F32, own)
                block = own.enter_context(nc.Block(no_gpsimd_drain=True))

                @block.vector
                def _(dve):
                    halves = halfmax[:].rearrange("p (t u) -> p t u", u=2)
                    nc.vector.tensor_tensor(rowmax[:], halves[:, :, 0], halves[:, :, 1], ALU.max).then_inc(joined, 1)
                    dve.wait_ge(joined, 1)
                    for b in range(8):
                        if b >= 2:
                            dve.wait_ge(spread, b - 1)
                        nc.vector.tensor_tensor(diag[:, b % 2], ident[:].unsqueeze(1).broadcast_to((P, 4, P)),
                                                bcast(rowmax[:, 4 * b:4 * b + 4], P), ALU.mult).then_inc(made, 1)

                @block.tensor
                def _(pe):
                    for b in range(8):
                        pe.wait_ge(made, b + 1)
                        pe.matmul(ps[:, b, :], ones[:], diag[:, b % 2].rearrange("p t f -> p (t f)"),
                                  start=True, stop=True).then_inc(spread, 1)

                @block.scalar
                def _(act):
                    for b in range(8):
                        act.wait_ge(spread, b + 1)
                        nc.scalar.copy(mb[:, b * BANK:(b + 1) * BANK], ps[:, b, :]).then_inc(copied, 1)

        def attend(x, HlT, HrT, mb):
            B = N // BANK
            BANKS = 4
            R = 8
            LAG = 4
            SUM_LAG = 2
            Z_AT, O_AT, END_AT = LAG + 1, LAG + 3, LAG + 6
            SIGN, NUMBER = ((9, 10), (12, 13), (26, 27)), ((11, 13), (15, 18), (28, 31))
            ADD, FIND = ((17, 18), (23, 24), (T + 5, T + 7)), (20, 26, T + 9)
            st_ready, pt_ready, sum_even, sum_odd, sum_both, sum_read, pv_done, s_ready = (
                sem(f"at_{n}") for n in ("st_ready", "pt_ready", "sum_even", "sum_odd", "sum_both", "sum_read",
                                         "pv_done", "s_ready"))
            bt_copied, z_ready, z_copied, o_ready, o_used, own_v = (
                sem(f"at_{n}") for n in ("bt_copied", "z_ready", "z_copied", "o_ready", "o_used", "own"))
            with ExitStack() as own:
                pt = sb("pt", [P, R, BANK], F32, own)
                sumP = sb("sumP", [P, 2, BANK], F32, own)
                sumF = sb("sumF", [P, BANK], F32, own)
                btS = sb("btS", [P, BANK], F32, own)
                zS = sb("zS", [P, BANK], F32, own)
                rl = sb("rl", [P, 4], F32, own)
                w4 = sb("w4", [P, 4, P], F32, own)
                lists.place("at", own)
                block = own.enter_context(nc.Block(no_gpsimd_drain=True))

                def turn_of(slot, ig):
                    return ig + (EARLY // 2 if slot < 2 else 0)

                def listing(s, first, at):
                    for slot in range(lists.SLOTS):
                        for part in range(2):
                            if at[slot][part] % T == s and not (first and at[slot][part] >= T):
                                yield slot, part, at[slot][part] // T

                def run(eng, steps, last):
                    steps(0, True)
                    with eng.Fori(1, B) as ig:
                        steps(ig, False)
                    last()

                @block.sync
                def _(sp):
                    with sp.Fori(0, B) as ig:
                        for s in range(lists.SLOTS):
                            lists.load(sp, s, ig * 3 + s + EARLY, turn_of(s, ig))

                @block.gpsimd
                def _(pool):
                    def steps(ig, first):
                        for s in range(T):
                            j = s - SUM_LAG
                            if j % 2 == 1 and j != 1 and not (first and j < 0):
                                wait_apart(pool, pt_ready, ig * T + j + 1, passed_pool)
                                k = ig * (T // 2) + (j - 1) // 2
                                if j == 3:
                                    if not first:
                                        wait_apart(pool, sum_both, ig, passed_pool)
                                    nc.gpsimd.tensor_tensor(sumP[:, 1, :], pt[:, 1, :], pt[:, 3, :], ALU.add
                                                            ).then_inc(sum_odd, 2)
                                else:
                                    wait_apart(pool, sum_odd, k, passed_pool)
                                    nc.gpsimd.tensor_tensor(sumP[:, 1, :], sumP[:, 1, :], pt[:, j % R, :], ALU.add
                                                            ).then_inc(sum_odd, 1)
                            for slot, part, ago in listing(s, first, NUMBER):
                                lists.number(pool, slot, (ig - ago) * 3 + slot + EARLY, turn_of(slot, ig - ago), part)

                    def last():
                        for j in range(T - SUM_LAG, T):
                            if j % 2 == 1:
                                pool.wait_ge(pt_ready, (B - 1) * T + j + 1)
                                pool.wait_ge(sum_odd, (B - 1) * (T // 2) + (j - 1) // 2)
                                nc.gpsimd.tensor_tensor(sumP[:, 1, :], sumP[:, 1, :], pt[:, j % R, :], ALU.add
                                                        ).then_inc(sum_odd, 1)

                    run(pool, steps, last)

                @block.tensor
                def _(pe):
                    def project_z(ig):
                        pe.wait_ge(bt_copied, ig + 2)
                        pe.matmul(ps[:, 5, :], wh[:], btS[:], start=True, stop=True).then_inc(z_ready, 1)

                    def project_o(ig):
                        pe.wait_ge(o_used, ig + 1)
                        pe.wait_ge(sum_both, ig + 1)
                        for k in range(4):
                            ins = pe.matmul(ps[:, 7, k:k + 1], sumF[:, k * P:(k + 1) * P], ones[:, 0:1],
                                            start=True, stop=True)
                        ins.then_inc(sum_read, 1)
                        pe.wait_ge(z_copied, ig + 1)
                        for k in range(4):
                            ins = pe.matmul(ps[:, 6, k * P:(k + 1) * P], zS[:, k * P:(k + 1) * P], wg[:],
                                            start=True, stop=True)
                        ins.then_inc(o_ready, 1)

                    def steps(ig, first):
                        for s in range(T):
                            pe.wait_ge(st_ready, ig * T + s + 1)
                            pe.matmul(ps[:, s % BANKS, :], HrT[:, s * P:(s + 1) * P],
                                      HlT[:, bass.ds(ig * BANK, BANK)], start=True, stop=True).then_inc(s_ready, 1)
                            j = s - LAG
                            if not (first and j < 0):
                                pe.wait_ge(pt_ready, ig * T + j + 1)
                                if j == 0:
                                    pe.wait_ge(bt_copied, ig + 1)
                                pe.matmul(ps[:, 4, :], x[:, j % T, :], pt[:, j % R, :], start=j == 0,
                                          stop=j % T == T - 1).then_inc(pv_done, 1)
                            if s == Z_AT and not first:
                                project_z(ig - 1)
                            if s == O_AT and not first:
                                project_o(ig - 1)

                    def last():
                        for j in range(T - LAG, T):
                            pe.wait_ge(pt_ready, (B - 1) * T + j + 1)
                            pe.matmul(ps[:, 4, :], x[:, j, :], pt[:, j % R, :], start=False, stop=j == T - 1
                                      ).then_inc(pv_done, 1)
                        project_z(B - 1)
                        project_o(B - 1)

                    pe.sem_inc(pv_done, R)
                    pe.sem_inc(sum_read, 1)
                    run(pe, steps, last)

                @block.scalar
                def _(act):
                    def keep_bt(ig):
                        act.wait_ge(pv_done, ig * T + T + R)
                        nc.scalar.copy(btS[:], ps[:, 4, :]).then_inc(bt_copied, 1)

                    def keep_z(ig):
                        act.wait_ge(z_ready, ig + 1)
                        nc.scalar.copy(zS[:], ps[:, 5, :]).then_inc(z_copied, 1)

                    def list_steps(s, ig, first):
                        for slot, part, ago in listing(s, first, ADD):
                            lists.add(act, slot, (ig - ago) * 3 + slot + EARLY, turn_of(slot, ig - ago), part)
                        for slot, part, ago in listing(s, first, SIGN):
                            lists.sign(act, slot, turn_of(slot, ig - ago), part)

                    def steps(ig, first):
                        for s in range(T):
                            if s == LAG - 1 and not first:
                                keep_bt(ig - 1)
                            if s == O_AT and not first:
                                keep_z(ig - 1)
                            act.wait_ge(st_ready, ig * T + s + 1 + BANKS)
                            nc.scalar.activation(pt[:, s % R, :], pt[:, s % R, :], ACT.Exp).then_inc(pt_ready, 1)
                            list_steps(s, ig, first)

                    def last():
                        keep_bt(B - 1)
                        lists.add(act, 2, (B - 1) * 3 + 2 + EARLY, turn_of(2, B - 1), 0)
                        keep_z(B - 1)
                        lists.add(act, 2, (B - 1) * 3 + 2 + EARLY, turn_of(2, B - 1), 1)

                    act.sem_inc(bt_copied, 1)
                    run(act, steps, last)

                @block.vector
                def _(dve):
                    def add_even(ig, j):
                        k = ig * (T // 2) + j // 2
                        if j == 0:
                            return
                        dve.wait_ge(pt_ready, ig * T + j + 1)
                        if j == 2:
                            nc.vector.tensor_tensor(sumP[:, 0, :], pt[:, 0, :], pt[:, 2, :], ALU.add
                                                    ).then_inc(sum_even, 2)
                        else:
                            dve.wait_ge(sum_even, k + R // 2)
                            nc.vector.tensor_tensor(sumP[:, 0, :], sumP[:, 0, :], pt[:, j % R, :], ALU.add
                                                    ).then_inc(sum_even, 1)

                    def add_both(ig):
                        dve.wait_ge(sum_even, (ig + 1) * (T // 2) + R // 2)
                        dve.wait_ge(sum_odd, (ig + 1) * (T // 2))
                        dve.wait_ge(sum_read, ig + 1)
                        nc.vector.tensor_tensor(sumF[:], sumP[:, 0, :], sumP[:, 1, :], ALU.add).then_inc(sum_both, 1)
                        dve.wait_ge(sum_both, ig + 1)

                    def end(ig):
                        tiles = bass.ds(ig * 4, 4)
                        dve.wait_ge(o_ready, ig + 1)
                        nc.vector.reciprocal(rl[:], ps[:, 7, 0:4]).then_inc(own_v, 1)
                        dve.wait_ge(own_v, ig * 3 + 1)
                        nc.vector.tensor_scalar(rl[:], rl[:], gam[:, 0:1], None, ALU.mult).then_inc(own_v, 1)
                        dve.wait_ge(own_v, ig * 3 + 2)
                        nc.vector.tensor_tensor(w4[:], ps[:, 6, :].rearrange("p (t f) -> p t f", f=P),
                                                bcast(rl[:], P), ALU.mult).then_inc(o_used, 1)
                        dve.wait_ge(o_used, ig + 2)
                        nc.vector.tensor_tensor(res[:, tiles, :], w4[:], x[:, tiles, :], ALU.add).then_inc(own_v, 1)
                        dve.wait_ge(own_v, ig * 3 + 3)

                    def find(s, ig, first):
                        for slot in range(lists.SLOTS):
                            for ago in range(2):
                                part = s + ago * T - FIND[slot]
                                if 0 <= part < lists.PARTS and not (first and ago):
                                    lists.find(dve, slot, (ig - ago) * 3 + slot + EARLY, turn_of(slot, ig - ago),
                                               [part])

                    def steps(ig, first):
                        for s in range(T):
                            dve.wait_ge(s_ready, ig * T + s + 1)
                            dve.wait_ge(pv_done, ig * T + s + 1)
                            if s % 2 == 0:
                                dve.wait_ge(sum_even, ig * (T // 2) + s // 2 + 1)
                            elif not (first and s < R):
                                dve.wait_ge(sum_odd, ig * (T // 2) + (s - R) // 2 + 1)
                            nc.vector.tensor_tensor(pt[:, s % R, :], ps[:, s % BANKS, :],
                                                    mb[:, bass.ds(ig * BANK, BANK)], ALU.subtract
                                                    ).then_inc(st_ready, 1)
                            j = s - SUM_LAG
                            if s == SUM_LAG + 1 and not first:
                                add_both(ig - 1)
                            if j % 2 == 0 and not (first and j < 0):
                                add_even(ig, j)
                            find(s, ig, first)
                            if s == END_AT and not first:
                                end(ig - 1)

                    def last():
                        for j in range(T - SUM_LAG, T):
                            if j % 2 == 0:
                                add_even(B - 1, j)
                        add_both(B - 1)
                        for slot in range(lists.SLOTS):
                            if slot == 2:
                                end(B - 1)
                            parts = range(max(0, T - FIND[slot]), lists.PARTS)
                            lists.find(dve, slot, (B - 1) * 3 + slot + EARLY, turn_of(slot, B - 1), parts)

                    dve.sem_inc(st_ready, BANKS)
                    dve.sem_inc(sum_even, R // 2)
                    dve.sem_inc(o_used, 1)
                    run(dve, steps, last)

        with ExitStack() as own:
            HlT = sb("HlT", [P, N], F32, own)
            HrT = sb("HrT", [P, N], F32, own)
            numbers = sb("numbers", [P, N], F32, own)
            with ExitStack() as inner:
                HT = sb("HT", [P, N], F32, inner)
                project(xb, HT, HlT, HrT)
            mb = sb("mb", [P, N], F32, own)
            halfmax = sb("halfmax", [P, 2 * T], F32, own)
            row_maxima(HlT, HrT, halfmax)
            spread_maxima(halfmax, mb)
            attend(xb, HlT, HrT, mb)

        class Settler:

            def __init__(self, own):
                self.own_v, self.total, self.summed = sem("sl_own"), sem("sl_total"), sem("sl_summed")
                self.n = Count()
                self.listed = sb("sl_listed", [P, T], F32, own)
                self.summed_keys = sb("sl_summed_keys", [P, T], F32, own)
                self.over = sb("sl_over", [P, T], F32, own)
                self.bad = sb("sl_bad", [P, 2 + len(TIERS)], F32, own)
                self.chosen = sb("sl_chosen", [P, len(TIERS), 8], F32, own)
                self.spare = sb("sl_spare", [P, T, K], F32, own)
                self.picked = sb("sl_picked", [P, E, W], F32, own)
                self.sel = sb("sl_sel", [P, W, T], F32, own)

            def settle(self, dve):
                own_v, n, bad, over = self.own_v, self.n, self.bad, self.over

                def rows(dst, src, spare):
                    nc.vector.tensor_scalar(spare, src, 0.0, float(N + 1), ALU.is_equal, ALU.mult
                                            ).then_inc(own_v, n.up())
                    dve.wait_ge(own_v, n.now)
                    nc.vector.tensor_tensor(spare, spare, src, ALU.add).then_inc(own_v, n.up())
                    dve.wait_ge(own_v, n.now)
                    nc.vector.tensor_scalar(dst, spare, -1.0, None, ALU.add).then_inc(own_v, n.up())
                    dve.wait_ge(own_v, n.now)

                nc.vector.memset(self.picked[:], 0.0).then_inc(own_v, n.up())
                nc.vector.tensor_reduce(self.listed[:], keys[:], AX.X, ALU.add).then_inc(own_v, n.up())
                nc.vector.tensor_tensor(self.summed_keys[:], keysum[:, :, 0], keysum[:, :, 1], ALU.add
                                        ).then_inc(own_v, n.up())
                dve.wait_ge(own_v, n.now)
                nc.vector.tensor_tensor(self.listed[:], self.listed[:], self.summed_keys[:], ALU.not_equal
                                        ).then_inc(own_v, n.up())
                dve.wait_ge(own_v, n.now)
                nc.vector.tensor_reduce(bad[:, 0:1], self.listed[:], AX.X, ALU.add).then_inc(own_v, n.up())
                for i, (start, to, room) in enumerate(TIERS):
                    nc.vector.tensor_scalar(over[:], keys[:, :, start], 0.0, None, ALU.is_gt).then_inc(own_v, n.up())
                    dve.wait_ge(own_v, n.now)
                    nc.vector.tensor_reduce(bad[:, 1 + i:2 + i], over[:], AX.X, ALU.add).then_inc(own_v, n.up())
                    dve.wait_ge(own_v, n.now)
                    nc.vector.tensor_scalar(bad[:, 1 + i:2 + i], bad[:, 1 + i:2 + i], float(room), None, ALU.is_gt
                                            ).then_inc(own_v, n.up())
                    nc.vector.tensor_tensor(over[:], over[:], tnum[:], ALU.mult).then_inc(own_v, n.up())
                    wait_apart(dve, own_v, n.now, passed)
                    nc.vector.max(self.chosen[:, i, :], over[:]).then_inc(own_v, n.up())
                    dve.wait_ge(own_v, n.now)
                    for r in range(room):
                        e = LISTS.index((i, r))
                        nc.vector.tensor_scalar(emask[:, e, :], tnum[:], self.chosen[:, i, r:r + 1], None,
                                                ALU.is_equal).then_inc(own_v, n.up())
                        dve.wait_ge(own_v, n.now)
                        sel = self.sel[:, 0:to - start, :]
                        nc.vector.tensor_tensor(sel, keys[:, :, start:to].rearrange("p t k -> p k t"),
                                                emask[:, e, :].unsqueeze(1).broadcast_to((P, to - start, T)),
                                                ALU.mult).then_inc(own_v, n.up())
                        dve.wait_ge(own_v, n.now)
                        nc.vector.tensor_reduce(self.picked[:, e, 0:to - start], sel, AX.X, ALU.add
                                                ).then_inc(own_v, n.up())
                        dve.wait_ge(own_v, n.now)
                rows(extra_idx[:], self.picked[:], self.spare[:, 0:E, 0:W])
                rows(main_idx[:, 0:T, :], keys[:, :, 0:K], self.spare[:])
                nc.vector.memset(main_idx[:, T:T + 2, :], 0).then_inc(own_v, n.up())
                nc.vector.tensor_scalar(diag_sb[:], diag_sb[:], 0.0, None, ALU.not_equal).then_inc(own_v, n.up())
                dve.wait_ge(own_v, n.now)
                nc.vector.tensor_tensor(count[:], diag_sb[:], keys[:, :, 0], ALU.add).then_inc(own_v, n.up())
                last = 1 + len(TIERS)
                nc.vector.tensor_reduce(bad[:, last:last + 1], bad[:, 0:last], AX.X, ALU.add).then_inc(self.summed, 1)

            def total_up(self, pe):
                pe.wait_ge(self.summed, 1)
                last = 1 + len(TIERS)
                pe.matmul(ps[:, 7, 0:1], ones[:], self.bad[:, last:last + 1], start=True, stop=True
                          ).then_inc(self.total, 1)

            def decide(self, dve):
                dve.wait_ge(self.total, 1)
                nc.vector.tensor_scalar(ok[:], ps[:, 7, 0:1], 0.0, None, ALU.is_equal).then_inc(self.own_v, self.n.up())
                dve.wait_ge(self.own_v, self.n.now)

        def finish1(dve, g, turn, y, y_used, v_own, n, work, stats, mv, rstd, root, done):
            tiles = bass.ds(g * TG, TG)
            nc.vector.tensor_tensor(work[:, 0], y, res[:, tiles, :], ALU.add).then_inc(y_used, 1)
            dve.wait_ge(y_used, turn + 2)
            normalize(dve, v_own, n, work, stats, mv, rstd, root, xa[:, tiles, :])

        def finish2(dve, g, turn, y, y_used, v_own, n, work, stats, mv, rstd, root, done):
            tiles = bass.ds(g * TG, TG)
            nc.vector.tensor_tensor(work[:, 0], y, bias2b[:].unsqueeze(1).broadcast_to((P, TG, P)), ALU.add
                                    ).then_inc(y_used, 1)
            dve.wait_ge(y_used, turn + 2)
            nc.vector.tensor_scalar(res[:, tiles, :], work[:, 0], 0.0, None, ALU.max).then_inc(done, 1)
            dve.wait_ge(done, g + 1)

        with ExitStack() as own:
            settler = Settler(own)
            aggregate("l12", [
                Layer(xb, ident, finish1, NORM_STEPS, dve_first=settler.settle, pe_last=settler.total_up,
                      dve_last=settler.decide),
                Layer(xa, w2, finish2, 0, norm=False, part_sums=colpart, store=(h_rows[0:N], res))])

        def inverse_of(dve, deg, inv, spare, v_own, n):
            nc.vector.tensor_scalar(spare[:], deg, 0.0, None, ALU.is_gt).then_inc(v_own, n.up())
            dve.wait_ge(v_own, n.now)
            nc.vector.tensor_tensor(inv[:], deg, spare[:], ALU.mult).then_inc(v_own, n.up())
            nc.vector.tensor_scalar(spare[:], spare[:], -1.0, 1.0, ALU.mult, ALU.add).then_inc(v_own, n.up())
            dve.wait_ge(v_own, n.now)
            nc.vector.tensor_tensor(inv[:], inv[:], spare[:], ALU.add).then_inc(v_own, n.up())
            dve.wait_ge(v_own, n.now)
            nc.vector.reciprocal(inv[:], inv[:]).then_inc(v_own, n.up())
            dve.wait_ge(v_own, n.now)

        def maxima_and_layer3():
            staged, gathered = ([sem(f"nm_{n}{s}") for s in range(2)] for n in ("staged", "gathered"))
            extra_in, extra_used = sem("nm_extra_in"), sem("nm_extra_used")
            row_loaded, spread, taken = ([sem(f"nm_{n}{s}") for s in range(2)] for n in
                                         ("row_loaded", "spread", "taken"))
            C = 2
            L = 4
            PARTS = [(product, half) for half in range(2) for product in range(2)]
            HALF = N // 2
            own_v, v_own, var_ready, std_ready, turned, turned_kept, made, own_n = (
                sem(f"nm_{n}") for n in ("own", "norm", "var_ready", "std_ready", "turned", "turned_kept", "made",
                                         "max_kept"))
            chunk_loaded = [sem(f"nm_chunk_loaded{c}") for c in range(L)]
            x_ready, xt_ready, chunk_used, part_used, y_ready, y_used, end_v = (
                sem(f"nm_{n}") for n in ("x_ready", "xt_ready", "chunk_used", "part_used", "y_ready", "y_used", "end"))
            out_scaled, out_added, end_var, end_std, scale_ready, finished, stored = (
                sem(f"nm_{n}") for n in ("out_scaled", "out_added", "end_var", "end_std", "scale_ready", "finished",
                                         "stored"))
            with ExitStack() as own:
                R = sb("nm_R", [P, T, P], F32, own)
                RT = R[:].rearrange("p t f -> p (t f)")
                got = sb("nm_got", [P, 2, K + E, P], F32, own)
                got_extra = sb("nm_got_extra", [P, max(map(len, STAGES)), W, P], F32, own)
                extra_most = sb("nm_extra_most", [P, E, P], F32, own)
                idx = sb("nm_idx", [P, 2, K], U32, own)
                most = sb("nm_most", [P, 2, P], F32, own)
                low = sb("nm_low", [P, T], F32, own)
                work = sb("nm_work", [P, 1, TG, P], F32, own)
                stats = sb("nm_stats", [P, TG, 6], F32, own)
                mv = sb("nm_mv", [P, TG, 2], F32, own)
                rstd = sb("nm_rstd", [P, TG], F32, own)
                stats2 = sb("nm_stats2", [P, 2, 6], F32, own)
                mv2 = sb("nm_mv2", [P, 2, 2], F32, own)
                rstd2 = sb("nm_rstd2", [P, 2], F32, own)
                chunks = sb("nm_chunks", [P, L, HALF], F32, own)
                dense_rows = chunks[:].rearrange("p (s u) w -> p s (u w)", u=2)
                y_out = sb("nm_y_out", [P, 2, 4, P], F32, own)
                xt = sb("nm_xt", [P, C, P], F32, own)
                acc = sb("nm_acc", [P, 2, N], F32, own)
                hT = acc[:, 0, :]
                mask = acc[:, 1, :].bitcast(BF16).rearrange("p (s n) -> p s n", s=2)
                junk = (got[:, 0, 0:16, :].rearrange("p k f -> p (k f)").bitcast(BF16)
                        .rearrange("p (u w) -> p u w", u=2))
                identb = sb("nm_identb", [P, P], BF16, own)
                pm = sb("nm_pm", [P, 2], F32, own)
                inv = sb("nm_inv", [P, 2, T], F32, own)
                end_scale = sb("nm_end_scale", [P, 2, 4], F32, own)
                end_shift = sb("nm_end_shift", [P, 2, 4], F32, own)
                coldeg = sb("nm_coldeg", [P, T], F32, own)
                spare = sb("nm_spare", [P, T], F32, own)
                block = own.enter_context(nc.Block(no_gpsimd_drain=True))

                def gather_listed(pool):
                    def gather_pair(it):
                        for h in range(2):
                            wait_apart(pool, staged[h], it + 1, passed_pool)
                            for k in range(K):
                                pool.indirect_dma_start(got[:, h, k, :], None, h_rows,
                                                        bass.IndirectOffsetOnAxis(idx[:, h, k:k + 1], 0)
                                                        ).then_inc(gathered[h], 16)

                    for p, stage in enumerate(STAGES):
                        if p:
                            pool.wait_ge(extra_used, p)
                        for i, e in enumerate(stage):
                            for k in range(EXTRA[e]):
                                pool.indirect_dma_start(got_extra[:, i, k, :], None, h_rows,
                                                        bass.IndirectOffsetOnAxis(extra_idx[:, e, k:k + 1], 0)
                                                        ).then_inc(extra_in, 16)
                        gather_pair(p)
                    with pool.Fori(len(STAGES), T // 2) as it:
                        gather_pair(it)

                def maxima_listed(dve):
                    n = Count()
                    for h in range(2):
                        nc.vector.tensor_copy(idx[:, h, :], main_idx[:, h, :]).then_inc(staged[h], 1)
                    nc.vector.memset(extra_most[:], 0.0).then_inc(own_v, n.up())
                    nc.vector.tensor_scalar(low[:], count[:], 0.0, LOWEST, ALU.is_equal, ALU.mult
                                            ).then_inc(own_v, n.up())
                    nc.vector.tensor_tensor(R[:], res[:], bcast(diag_sb[:], P), ALU.mult).then_inc(own_v, n.up())
                    dve.wait_ge(own_v, n.now)
                    clear_sums(dve, n)
                    base, steps = n.now, 2 * 2 + 3 - 1 + 1

                    def pair(it, add):
                        m, q = Count(base + it * 8), Count(it * steps)
                        for h in range(2):
                            t = it * 2 + h
                            nc.vector.tensor_tensor(got[:, h, K:K + E, :], extra_most[:],
                                                    emask[:, :, bass.ds(t, 1)].broadcast_to((P, E, P)), ALU.mult
                                                    ).then_inc(own_v, m.up())
                            if h == 1:
                                add(1)
                            dve.wait_ge(own_v, m.now)
                            dve.wait_ge(gathered[h], (it + 1) * (16 * K))
                            nc.vector.tensor_reduce(most[:, h, :], got[:, h].rearrange("p k f -> p f k"),
                                                    AX.X, ALU.max).then_inc(own_v, m.up())
                            dve.wait_ge(own_v, m.now)
                            nc.vector.tensor_copy(idx[:, h, :].unsqueeze(1), main_idx[:, bass.ds(t + 2, 1), :]
                                                  ).then_inc(staged[h], 1)
                            tile = R[:, bass.ds(t, 1), :]
                            nc.vector.tensor_tensor(tile, tile, most[:, h, :].unsqueeze(1), ALU.max
                                                    ).then_inc(own_v, m.up())
                            dve.wait_ge(own_v, m.now)
                            nc.vector.tensor_scalar(work[:, 0, h, :].unsqueeze(1), tile, low[:, bass.ds(t, 1)], None,
                                                    ALU.add).then_inc(own_v, m.up())
                            if h == 0:
                                add(0)
                        dve.wait_ge(own_v, m.now)
                        tiles = bass.ds(it * 2, 2)
                        nc.vector.tensor_tensor(work[:, 0, 0:2], work[:, 0, 0:2], xa[:, tiles, :], ALU.add
                                                ).then_inc(v_own, q.up())
                        dve.wait_ge(v_own, q.now)
                        normalize(dve, v_own, q, work[:, :, 0:2], stats2, mv2, rstd2, (var_ready, std_ready, it + 1),
                                  xb[:, tiles, :], (x_ready, it + 1))
                        assert (m.n, q.n) == (8, steps), (m.n, q.n)
                        for part in range(2, len(PARTS)):
                            add(part)

                    for p, stage in enumerate(STAGES):
                        dve.wait_ge(extra_in, sum(16 * EXTRA[e] for e in sum(STAGES[:p + 1], [])))
                        for i, e in enumerate(stage):
                            ins = nc.vector.tensor_reduce(extra_most[:, e, :],
                                                          got_extra[:, i, 0:EXTRA[e], :].rearrange("p k f -> p f k"),
                                                          AX.X, ALU.max)
                        ins.then_inc(extra_used, 1)
                        dve.wait_ge(extra_used, p + 1)
                        pair(p, lambda part: add_part(dve, p - 1, part) if p > 0 else None)
                    with dve.Fori(len(STAGES), T // C) as block_no:
                        pair(block_no, lambda part: add_part(dve, block_no - 1, part))

                def add_part(dve, block_no, part):
                    product, half = PARTS[part]
                    n = block_no * len(PARTS) + part
                    dve.wait_ge(chunk_used, n * C + C + L)
                    to = acc[:, product, half * HALF:(half + 1) * HALF]
                    nc.vector.tensor_tensor(to, to, ps[:, 4 * (part % 2):4 * (part % 2) + 4, :]
                                            .rearrange("p b w -> p (b w)"), ALU.add).then_inc(part_used, 1)
                    dve.wait_ge(part_used, n + 3)

                def clear_sums(dve, n):
                    nc.vector.memset(acc[:], 0.0).then_inc(own_v, n.up())
                    dve.wait_ge(own_v, n.now)

                def root(act, g, of):
                    act.wait_ge(var_ready, g + 1)
                    nc.scalar.activation(of[:], of[:], ACT.Sqrt).then_inc(std_ready, 1)

                def load_chunks(sp):
                    streams = [m.rearrange("(n c p) (h w) -> c h n p w", c=C, p=P, w=HALF) for m in (adjT, adj)]
                    with sp.Fori(0, T // C) as block_no:
                        for part, (product, half) in enumerate(PARTS):
                            for c in range(C):
                                n, slot = block_no * (len(PARTS) * C) + part * C + c, (part * C + c) % L
                                sp.wait_ge(chunk_used, n + 1)
                                sp.dma_start(chunks[:, slot, :], streams[product][c, half, block_no]
                                             ).then_inc(chunk_loaded[slot], 16)

                def hold_tile(act, block_no, c):
                    if c == 0:
                        act.wait_ge(x_ready, block_no + 1)
                    act.wait_ge(chunk_used, block_no * (len(PARTS) * C) + c + 1 + L - C)
                    nc.scalar.copy(xt[:, c, :].unsqueeze(1), xb[:, bass.ds(block_no * C + c, 1), :]
                                   ).then_inc(xt_ready, 1)

                def sum_and_project(pe):
                    pe.sem_inc(chunk_used, L)
                    pe.sem_inc(part_used, 2)
                    turns = len(PARTS) * C // L

                    def sum_part(block_no, part, before=None):
                        pe.wait_ge(part_used, block_no * len(PARTS) + part + 1)
                        for c in range(C):
                            slot, turn = (part * C + c) % L, (part * C + c) // L
                            if part == 0:
                                pe.wait_ge(xt_ready, block_no * C + c + 1)
                            pe.wait_ge(chunk_loaded[slot], (block_no * turns + turn + 1) * 16)
                            for b in range(4):
                                if before is not None and c == 0:
                                    before(b)
                                ins = pe.matmul(ps[:, 4 * (part % 2) + b, :], xt[:, c, :],
                                                chunks[:, slot, b * BANK:(b + 1) * BANK],
                                                start=c == 0, stop=c == C - 1)
                            ins.then_inc(chunk_used, 1)

                    with pe.Fori(0, T // C - 1) as block_no:
                        for part in range(len(PARTS)):
                            sum_part(block_no, part)
                    last = T // C - 1
                    for part in range(3):
                        sum_part(last, part)
                    pe.wait_ge(part_used, last * len(PARTS) + 2 + 2)
                    for b in range(2):
                        project_four(pe, b)

                    def await_readers(b):
                        if b % 2 == 0:
                            pe.wait_ge(y_used, b // 2 + 1)
                            pe.wait_ge(out_scaled, (b // 2 + 1) * 4)

                    sum_part(last, 3, await_readers)
                    for b in range(2, 8):
                        if b < 6:
                            pe.wait_ge(part_used, last * len(PARTS) + 3 + b // 4 + 2)
                        else:
                            pe.wait_ge(y_used, b - 3)
                            pe.wait_ge(out_scaled, (b - 3) * 4)
                        project_four(pe, b)

                def y_banks(b):
                    return [ps[:, (2 * b + 4) % 8 + product, :].rearrange("p (t f) -> p t f", f=P)
                            for product in range(2)]

                def project_four(pe, b):
                    for product, right in enumerate((win, wout)):
                        for k in range(4):
                            t = 4 * b + k
                            ins = pe.matmul(y_banks(b)[product][:, k, :], acc[:, product, t * P:(t + 1) * P],
                                            right[:], start=True, stop=True)
                    ins.then_inc(y_ready, 1)

                def scale_out(act, b):
                    act.wait_ge(y_ready, b + 1)
                    if b >= 2:
                        act.wait_ge(out_added, b - 1)
                    for k in range(4):
                        t = 4 * b + k
                        nc.scalar.activation(y_out[:, b % 2, k, :], y_banks(b)[1][:, k, :], ACT.Copy,
                                             scale=inv[:, 1, t:t + 1]).then_inc(out_scaled, 1)

                def end_act(act):
                    for b in range(2):
                        scale_out(act, b)
                    for b in range(8):
                        act.wait_ge(end_var, b + 1)
                        scale = end_scale[:, b % 2, :]
                        nc.scalar.activation(scale, scale, ACT.Sqrt).then_inc(end_std, 1)
                        act.wait_ge(scale_ready, b + 1)
                        for k in range(4):
                            nc.scalar.activation(res[:, 4 * b + k, :], work[:, 0, b % 2 * 4 + k, :], ACT.Identity,
                                                 bias=end_shift[:, b % 2, k:k + 1], scale=scale[:, k:k + 1]
                                                 ).then_inc(finished, 1)
                        for next_b in {0: (), 1: (2, 3)}.get(b, (b + 2,)):
                            if next_b < 8:
                                scale_out(act, next_b)

                def end_dve(dve):
                    n = Count()
                    inverse_of(dve, rowdeg[:], inv[:, 0], spare, end_v, n)
                    nc.vector.tensor_reduce(coldeg[:], colpart[:].rearrange("p (g t) -> p t g", t=T), AX.X, ALU.add
                                            ).then_inc(end_v, n.up())
                    dve.wait_ge(end_v, n.now)
                    inverse_of(dve, coldeg[:], inv[:, 1], spare, end_v, n)

                    def take(b):
                        if b >= 2:
                            dve.wait_ge(finished, 4 * (b - 1))
                        dve.wait_ge(y_ready, b + 1)
                        for k in range(4):
                            t = 4 * b + k
                            ins = nc.vector.scalar_tensor_tensor(
                                out=work[:, 0, b % 2 * 4 + k, :], in0=y_banks(b)[0][:, k, :],
                                scalar=inv[:, 0, t:t + 1], in1=xb[:, t, :], op0=ALU.mult, op1=ALU.add)
                        ins.then_inc(y_used, 1)

                    def close(b):
                        w = work[:, :, b % 2 * 4:b % 2 * 4 + 4]
                        dve.wait_ge(y_used, b + 1)
                        dve.wait_ge(out_scaled, 4 * b + 4)
                        nc.vector.tensor_tensor(w[:, 0], w[:, 0], y_out[:, b % 2], ALU.add).then_inc(out_added, 1)
                        wait_apart(dve, out_added, b + 1, passed)
                        for k in range(4):
                            nc.vector.bn_stats(stats[:, k, :], w[:, 0, k, :]).then_inc(end_v, n.up())
                        wait_apart(dve, end_v, n.now, passed)
                        for k in range(4):
                            nc.vector.bn_aggr(mv[:, k, :], stats[:, k, :]).then_inc(end_v, n.up())
                        dve.wait_ge(end_v, n.now)
                        scale, shift = end_scale[:, b % 2, :], end_shift[:, b % 2, :]
                        nc.vector.tensor_scalar(scale, mv[:, 0:4, 1], EPS, None, ALU.add).then_inc(end_var, 1)
                        nc.vector.tensor_scalar(shift, mv[:, 0:4, 0], -1.0, None, ALU.mult).then_inc(end_v, n.up())
                        dve.wait_ge(end_std, b + 1)
                        nc.vector.reciprocal(scale, scale).then_inc(end_v, n.up())
                        dve.wait_ge(end_v, n.now)
                        nc.vector.tensor_tensor(shift, shift, scale, ALU.mult).then_inc(scale_ready, 1)

                    last = T // C - 1
                    add_part(dve, last, 0)
                    add_part(dve, last, 1)
                    take(0)
                    take(1)
                    add_part(dve, last, 2)
                    close(0)
                    close(1)
                    add_part(dve, last, 3)
                    for b in range(2, 8):
                        take(b)
                        close(b)

                def store(sp):
                    rows = out.rearrange("(b t p) f -> b p t f", t=4, p=P)
                    for b in range(8):
                        sp.wait_ge(finished, 4 * (b + 1))
                        sp.dma_start(rows[b], res[:, 4 * b:4 * b + 4, :]).then_inc(stored, 16)
                    sp.wait_ge(stored, 16 * 8)

                def load_rows(sp):
                    with sp.Fori(0, T // 2) as it:
                        for h in range(2):
                            sp.wait_ge(made, it * 4 + 2 * h + 1)
                            sp.dma_start(dense_rows[:, h, :], adj_rows[it * 2 + h]).then_inc(row_loaded[h], 16)
                    sp.wait_ge(made, 2 * T + 4)

                def keep_turned(act):
                    for b in range(8):
                        act.wait_ge(turned, b + 1)
                        nc.scalar.copy(hT[:, b * BANK:(b + 1) * BANK], ps[:, b, :]).then_inc(turned_kept, 1)

                def spread_masks(pe):
                    for b in range(8):
                        for k in range(4):
                            ins = pe.matmul(ps[:, b, k * P:(k + 1) * P], res[:, 4 * b + k, :], ident[:],
                                            start=True, stop=True)
                        ins.then_inc(turned, 1)
                    pe.wait_ge(turned_kept, 8)
                    with pe.Fori(0, T // 2) as it:
                        for h in range(2):
                            wait_apart(pe, made, it * 4 + 2 * h + 6, passed_pe)
                            with pe.Fori(0, P) as i:
                                n = (it * 2 + h) * P + i
                                for u in range(2):
                                    pe.wait_ge(taken[u], n + 1)
                                    for b in range(4 * u, 4 * u + 4):
                                        ins = pe.matmul(ps[:, b, :], identb[:, bass.ds(i, 1)].broadcast_to((P, P)),
                                                        mask[:, h, b * BANK:(b + 1) * BANK], start=True, stop=True)
                                    ins.then_inc(spread[u], 1)
                    pe.wait_ge(own_n, N)
                    for b in range(8):
                        for k in range(4):
                            t = 4 * b + k
                            ins = pe.matmul(ps[:, b, k * P:(k + 1) * P], RT[:, t * P:(t + 1) * P], ident[:],
                                            start=True, stop=True)
                        ins.then_inc(turned, 1)

                def maxima_dense(dve):
                    nc.vector.tensor_copy(identb[:], ident[:]).then_inc(made, 1)
                    dve.wait_ge(made, 1)
                    dve.sem_inc(made, 3)
                    dve.sem_inc(taken[0], 1)
                    dve.sem_inc(taken[1], 1)
                    dve.wait_ge(turned_kept, 8)
                    with dve.Fori(0, T // 2) as it:
                        for h in range(2):
                            t = it * 2 + h
                            dve.wait_ge(row_loaded[h], (it + 1) * 16)
                            nc.vector.tensor_scalar(mask[:, h, :], dense_rows[:, h, :], 0.0, None, ALU.not_equal
                                                    ).then_inc(made, 1)
                            dve.wait_ge(made, it * 4 + 2 * h + 5)
                            nc.vector.tensor_reduce(count[:, bass.ds(t, 1)], mask[:, h, :], AX.X, ALU.add
                                                    ).then_inc(made, 1)
                            wait_apart(dve, made, it * 4 + 2 * h + 6, passed)
                            with dve.Fori(0, P) as i:
                                n = t * P + i
                                for u in range(2):
                                    wait_apart(dve, spread[u], n + 1, passed)
                                    nc.vector.tensor_tensor_reduce(
                                        out=junk[:, u, :], in0=hT[:, u * (N // 2):(u + 1) * (N // 2)],
                                        in1=ps[:, 4 * u:4 * u + 4, :].rearrange("p b w -> p (b w)"),
                                        scale=1.0, scalar=0.0, op0=ALU.mult, op1=ALU.max,
                                        accum_out=pm[:, u:u + 1]).then_inc(taken[u], 1)
                                dve.wait_ge(taken[0], n + 2)
                                dve.wait_ge(taken[1], n + 2)
                                nc.vector.tensor_tensor(RT[:, bass.ds(n, 1)], pm[:, 0:1], pm[:, 1:2], ALU.max
                                                        ).then_inc(own_n, 1)
                                dve.wait_ge(own_n, n + 1)
                    n = Count()
                    clear_sums(dve, n)
                    nc.vector.tensor_scalar(low[:], count[:], 0.0, LOWEST, ALU.is_equal, ALU.mult
                                            ).then_inc(own_v, n.up())
                    dve.wait_ge(own_v, n.now)
                    for g in range(G):
                        tiles = slice(g * TG, (g + 1) * TG)
                        dve.wait_ge(turned, 8 + 2 * g + 2)
                        nc.vector.tensor_tensor(work[:, 0],
                                                ps[:, 2 * g:2 * g + 2, :].rearrange("p b (t f) -> p (b t) f", f=P),
                                                bcast(low[:, tiles], P), ALU.add).then_inc(own_v, n.up())
                        dve.wait_ge(own_v, n.now)
                        nc.vector.tensor_tensor(work[:, 0], work[:, 0], xa[:, tiles, :], ALU.add
                                                ).then_inc(own_v, n.up())
                        dve.wait_ge(own_v, n.now)
                        normalize(dve, own_v, n, work, stats, mv, rstd, (var_ready, std_ready, g + 1), xb[:, tiles, :])
                    dve.sem_inc(x_ready, T // 2)
                    with dve.Fori(0, T // C - 1) as block_no:
                        for part in range(len(PARTS)):
                            add_part(dve, block_no, part)

                @block.sync
                def _(sp):
                    lists_hold = sp.value_load(ok[0:1, 0:1])
                    with sp.If(lists_hold <= 0):
                        load_rows(sp)
                    load_chunks(sp)
                    store(sp)

                @block.tensor
                def _(pe):
                    lists_hold = pe.value_load(ok[0:1, 0:1])
                    with pe.If(lists_hold <= 0):
                        spread_masks(pe)
                    sum_and_project(pe)

                @block.gpsimd
                def _(pool):
                    lists_hold = pool.value_load(ok[0:1, 0:1])
                    with pool.If(lists_hold > 0):
                        gather_listed(pool)

                @block.scalar
                def _(act):
                    lists_hold = act.value_load(ok[0:1, 0:1])
                    with act.If(lists_hold <= 0):
                        keep_turned(act)
                        with act.Fori(0, G) as g:
                            root(act, g, rstd)
                        with act.Fori(0, T // C) as block_no:
                            for c in range(C):
                                hold_tile(act, block_no, c)
                    with act.Else():
                        with act.Fori(0, T // C) as block_no:
                            root(act, block_no, rstd2)
                            for c in range(C):
                                hold_tile(act, block_no, c)
                    end_act(act)

                @block.vector
                def _(dve):
                    lists_hold = dve.value_load(ok[0:1, 0:1])
                    with dve.If(lists_hold > 0):
                        maxima_listed(dve)
                    with dve.Else():
                        maxima_dense(dve)
                    end_dve(dve)

        maxima_and_layer3()


def kernel(x, adj, L0_gnn_kernel, L0_gnn_bias, L0_gnn_beta, L1_gnn_W_l, L1_gnn_W_r, L1_gnn_W_h, L1_gnn_W_g,
           L1_gnn_gamma, L2_gnn_weight, L2_gnn_bias, L3_gnn_W_in, L3_gnn_W_out):
    import numpy as np
    import concourse.bacc as bacc
    from concourse.bass_utils import run_bass_kernel_spmd

    x, adj = np.asarray(x), np.asarray(adj)
    N, D = x.shape
    tiled = x.reshape(N // P, P, D).transpose(1, 0, 2).reshape(P, -1)
    ins = {
        "adj": adj, "adjT": adj.T, "xin": tiled, "xT": x.T, "K0": L0_gnn_kernel,
        "bias0": np.asarray(L0_gnn_bias), "beta": np.asarray(L0_gnn_beta).reshape(N // P, P).T,
        "Wl": L1_gnn_W_l, "Wr": L1_gnn_W_r, "Wh": L1_gnn_W_h, "Wg": L1_gnn_W_g, "gamma": L1_gnn_gamma,
        "diag": np.diagonal(adj).reshape(N // P, P).T,
        "W2": L2_gnn_weight, "bias2": L2_gnn_bias, "Win": L3_gnn_W_in, "Wout": L3_gnn_W_out,
    }
    nc = bacc.Bacc("TRN2", target_bir_lowering=False, num_devices=1)
    arrays, args = {}, {}
    for name, a in ins.items():
        a = np.ascontiguousarray(a)
        arrays[f"in_{name}"] = a
        args[name] = nc.dram_tensor(f"in_{name}", a.shape, mybir.dt.from_np(a.dtype), kind="ExternalInput").ap()
    out = nc.dram_tensor("out_x", (N, D), F32, kind="ExternalOutput").ap()
    build(nc, out=out, **args)
    r = run_bass_kernel_spmd(nc, [arrays], core_ids=[0])
    return r.results[0]["out_x"]
```
